# Optimizing a Trainium2 kernel written in Bass

```python
import numpy as np
import jax
import jax.numpy as jnp

def _softmax(x, axis=-1):
    return jax.nn.softmax(x, axis=axis)

def _gelu(x):
    return jax.nn.gelu(x, approximate=True)

def _silu(x):
    return jax.nn.silu(x)

def _sigmoid(x):
    return jax.nn.sigmoid(x)

def _layernorm(x, axis=-1, eps=1e-05):
    m = jnp.mean(x, axis=axis, keepdims=True)
    v = jnp.var(x, axis=axis, keepdims=True)
    return (x - m) / jnp.sqrt(v + eps)

def _scatter_add(tgt, idx, src, axis=0):
    return tgt.at[idx].add(src)

def _segment_sum(src, seg, n):
    return jax.ops.segment_sum(src, seg, n)
kernel_name = 'mk_adj_preln_d2_adj_r2_d45499'

def setup_inputs(seed: int=0):
    np.random.seed(seed)
    _w = jnp.asarray

    def _rec_inputs():
        import jax
        import jax.numpy as jnp
        _gk = jax.random.key(seed)
        x = -8.776e-05 + 1 * jax.random.normal(jax.random.fold_in(_gk, 1), (10000, 128), jnp.float32)
        _a = jax.random.bernoulli(jax.random.fold_in(_gk, 2), 0.0016, (10000, 10000))
        _a = jnp.logical_or(_a, jnp.eye(10000, dtype=bool))
        _af = _a.astype(jnp.float32)
        _af = _af * jax.random.uniform(jax.random.fold_in(_gk, 3), (10000, 10000), jnp.float32, 0.05, 1)
        adj = _af
        return (x, adj)
    x, adj = _rec_inputs()

    def _L0_gnn_setup():
        import jax, jax.numpy as jnp
        import numpy as np
        N_USER = 10000
        N_ITEM = 10000
        HID = 128
        key = jax.random.key(seed)
        k1, k2, k3, k4, k5, k6, k7 = jax.random.split(key, 7)
        scale = 1.0 / np.sqrt(HID)
        return {'user_feat': jax.random.normal(k1, (N_USER, HID), dtype=jnp.float32), 'item_feat': jax.random.normal(k2, (N_ITEM, HID), dtype=jnp.float32), 'adj': jax.random.uniform(k3, (N_USER, N_ITEM), dtype=jnp.float32), 'W_item': jax.random.uniform(k4, (HID, HID), dtype=jnp.float32, minval=-scale, maxval=scale), 'b_item': jax.random.uniform(k5, (HID,), dtype=jnp.float32, minval=-scale, maxval=scale), 'W_user': jax.random.uniform(k6, (HID, HID), dtype=jnp.float32, minval=-scale, maxval=scale), 'b_user': jax.random.uniform(k7, (HID,), dtype=jnp.float32, minval=-scale, maxval=scale)}
    _L0_gnn_all = _L0_gnn_setup()
    _L0_gnn_in = {k: v for k, v in _L0_gnn_all.items() if k in ('item_feat', 'W_item', 'b_item', 'W_user', 'b_user')}
    del _L0_gnn_all

    def _L1_gnn_setup():
        import jax, jax.numpy as jnp
        import numpy as np
        key = jax.random.key(seed)
        k1, k2, k3, k4 = jax.random.split(key, 4)
        N, F_in, F_out = (4096, 128, 128)
        x = jax.random.normal(k1, (N, F_in), dtype=jnp.float32)
        adj = jax.random.uniform(k2, (N, N), dtype=jnp.float32)
        lim = 1.0 / np.sqrt(F_in)
        W = jax.random.uniform(k3, (F_out, F_in), dtype=jnp.float32, minval=-lim, maxval=lim)
        b = jax.random.uniform(k4, (F_out,), dtype=jnp.float32, minval=-lim, maxval=lim)
        return {'x': x, 'adj': adj, 'W': W, 'b': b}
    _L1_gnn_all = _L1_gnn_setup()
    _L1_gnn_in = {k: v for k, v in _L1_gnn_all.items() if k in ('W', 'b')}
    del _L1_gnn_all
    return {'x': x, 'adj': adj, 'L0_gnn_item_feat': _L0_gnn_in['item_feat'], 'L0_gnn_W_item': _L0_gnn_in['W_item'], 'L0_gnn_b_item': _L0_gnn_in['b_item'], 'L0_gnn_W_user': _L0_gnn_in['W_user'], 'L0_gnn_b_user': _L0_gnn_in['b_user'], 'L1_gnn_W': _L1_gnn_in['W'], 'L1_gnn_b': _L1_gnn_in['b']}

def reference(x, adj, L0_gnn_item_feat, L0_gnn_W_item, L0_gnn_b_item, L0_gnn_W_user, L0_gnn_b_user, L1_gnn_W, L1_gnn_b):
    import jax
    import jax.numpy as jnp

    def _L0_gnn_ref(user_feat, item_feat, adj, W_item, b_item, W_user, b_user):
        import jax, jax.numpy as jnp
        import numpy as np
        N_USER = 10000
        N_ITEM = 10000
        HID = 128
        h = item_feat @ W_item.T + b_item
        b = user_feat @ W_user.T + b_user
        return jax.nn.relu(adj @ h + b)

    def _L1_gnn_ref(x, adj, W, b):
        import jax, jax.numpy as jnp
        import numpy as np
        N = adj.shape[0]
        adj = adj + jnp.eye(N, dtype=adj.dtype)
        deg = adj.sum(axis=1)
        deg_inv_sqrt = deg ** (-0.5)
        deg_inv_sqrt = jnp.where(jnp.isinf(deg_inv_sqrt), 0.0, deg_inv_sqrt)
        adj_normalized = deg_inv_sqrt[:, None] * adj * deg_inv_sqrt[None, :]
        support = x @ W.T + b
        return adj_normalized @ support
    h = jnp.maximum(_layernorm(x, axis=-1), 0.0)
    x = x + _L0_gnn_ref(h, L0_gnn_item_feat, adj, L0_gnn_W_item, L0_gnn_b_item, L0_gnn_W_user, L0_gnn_b_user)
    h = jnp.maximum(_layernorm(x, axis=-1), 0.0)
    x = x + _L1_gnn_ref(h, adj, L1_gnn_W, L1_gnn_b)
    return x

_drawn_inputs = setup_inputs


def setup_inputs(seed=0):
    import zlib

    import numpy as np

    out = dict(_drawn_inputs(seed))
    spreads = {}
    factors = {}
    for name, (base, spread) in spreads.items():
        noise = np.random.default_rng([zlib.crc32(name.encode()), seed]).standard_normal(out[name].shape)
        drawn = base * np.exp(spread * noise) if base else spread * noise
        out[name] = jnp.asarray(drawn.astype(out[name].dtype))
    for name, factor in factors.items():
        out[name] = (out[name] * factor).astype(out[name].dtype)
    return out
```

```python
import concourse.bass as bass
from concourse import mybir
from contextlib import ExitStack

F32 = mybir.dt.float32
ALU = mybir.AluOpType
ACT = mybir.ActivationFunctionType

N = 10000
F = 128
ROWS = 125
CHUNKS = 4
BLOCK = ROWS * CHUNKS
BLOCKS = N // BLOCK
GROUP = CHUNKS * BLOCK
SECTION = 4
SECTIONS = BLOCKS // SECTION
SLOTS = 4
PER_SLOT = BLOCKS // SLOTS
LN_EPS = 1e-5


def done(n):
    return n + 1


def stored(n):
    return 16 * (n + 1)


def loaded(n):
    return 16 * n


def wait_alone(eng, semaphore, value, passed):
    eng.wait_ge(semaphore, value)
    eng.sem_inc(passed, 1)


def column_blocks(section):
    first = SECTION * section
    return list(range(first, BLOCKS)) + list(range(first))


def loads_before(section_index):
    return PER_SLOT * BLOCKS + SECTION * section_index * (section_index + 1) // 2


def gnn_two_layers(nc, x, adj_t, item_t, w_item_t, b_item4, w_user_t, b_user, w_out_t, b_out4, out):
    ctx = ExitStack()
    with ctx:
        def sb(name, shape, dt=F32):
            return ctx.enter_context(nc.sbuf_tensor(name, shape, dt))

        def bank(name):
            return ctx.enter_context(nc.psum_tensor(name, [128, 512], F32))

        def sem(name):
            return ctx.enter_context(nc.semaphore(name))

        x1_dram = nc.dram_tensor("x1_dram", (BLOCKS, ROWS, CHUNKS * F), F32, kind="Internal").ap()
        part_dram = nc.dram_tensor("part_dram", (BLOCKS, F, BLOCK), F32, kind="Internal").ap()

        h_sb = sb("h_sb", [ROWS, BLOCKS * CHUNKS * F])
        s_sb = sb("s_sb", [ROWS, BLOCKS * CHUNKS * F])
        d_sb = sb("d_sb", [ROWS, BLOCKS * CHUNKS])
        adj_sb = [sb(f"adj{i}", [128, GROUP]) for i in range(SLOTS)]
        acc = sb("acc", [ROWS, GROUP])
        fold = sb("fold", [ROWS, BLOCK])

        ident = sb("ident", [128, 128])
        ones_col = sb("ones_col", [128, 1])
        ones_row = sb("ones_row", [1, 128])
        minus_half = sb("minus_half", [ROWS, CHUNKS])
        wi = sb("wi", [F, F])
        wu = sb("wu", [F, F])
        wo = sb("wo", [F, F])
        bu = sb("bu", [F, 1])
        b_rows = sb("b_rows", [1, 2 * CHUNKS * F])
        bi_all = sb("bi_all", [ROWS, CHUNKS * F])
        bo_all = sb("bo_all", [ROWS, CHUNKS * F])
        item_sb = [sb(f"item{i}", [F, BLOCK]) for i in range(2)]

        xu = sb("xu", [ROWS, CHUNKS, F])
        xn = sb("xn", [ROWS, CHUNKS, F])
        xr = sb("xr", [ROWS, CHUNKS, F])
        x1 = sb("x1", [ROWS, CHUNKS, F])
        h2 = sb("h2", [ROWS, CHUNKS, F])
        sup = sb("sup", [ROWS, CHUNKS, F])
        u_t = sb("u_t", [F, BLOCK])
        r_t = sb("r_t", [F, BLOCK])
        h2_t = sb("h2_t", [F, BLOCK])
        part = sb("part", [F, BLOCK])
        stats = {k: sb(f"stats_{k}", [ROWS, CHUNKS, 6]) for k in "u2"}
        mv = {k: sb(f"mv_{k}", [ROWS, CHUNKS, 2]) for k in "u2"}
        var = {k: sb(f"var_{k}", [ROWS, CHUNKS]) for k in "u2"}
        rstd = {k: sb(f"rstd_{k}", [ROWS, CHUNKS]) for k in "u2"}
        deg0 = sb("deg0", [ROWS, CHUNKS])
        deg1 = sb("deg1", [ROWS, CHUNKS])
        dpow = sb("dpow", [ROWS, CHUNKS])
        dcur = sb("dcur", [ROWS, CHUNKS])

        z1, z2, ps_u, ps_r, ps_h, ps_s, ps_d = (bank(n) for n in ("z1", "z2", "ps_u", "ps_r", "ps_h", "ps_s", "ps_d"))
        z_banks = [z1, z2]

        consts_in = sem("consts_in")
        consts_set = sem("consts_set")
        ident_zero = sem("ident_zero")
        item_in = [sem(f"item_in{i}") for i in range(2)]
        bias_mm = sem("bias_mm")
        bias_done = sem("bias_done")
        h_mm = sem("h_mm")
        h_done = sem("h_done")
        adj_in = [sem(f"adj_in{i}") for i in range(SLOTS)]
        pe_groups = sem("pe_groups")
        row_sums = sem("row_sums")
        waits_passed = sem("waits_passed")

        STAGES = ("u_stats", "u_aggr", "u_var", "u_rstd", "u_norm", "u_turned", "u_relu", "u_added",
                  "z1_summed", "r_relu", "r_turned", "x1_made", "l2_stats", "l2_aggr", "l2_var", "l2_rstd",
                  "h2_norm", "h2_turned", "h2_relu", "sup_mm", "sup_bias", "s_made",
                  "fold_half", "fold_made", "deg_mm", "deg_zero", "deg_safe", "deg_pow", "d_cur", "d_made",
                  "part_made", "zt_made", "zt_turned", "zs_added", "out_made")
        STAGES_DMA = ("xu_in", "xr_in", "x1_stored", "part_stored", "part_in", "x1_in", "out_stored")
        S = {n: sem(n) for n in STAGES + STAGES_DMA}

        block = ctx.enter_context(nc.Block())

        def first_pass(eng, body):
            body(0, 0, True)
            for section in range(SECTIONS):
                with eng.Fori(max(1, SECTION * section), SECTION * (section + 1)) as b:
                    body(b, section, False)

        def second_pass(eng, body):
            for t in range(SECTION):
                body(t, 0, t == 0, t % 2)
            for v in range(1, SECTIONS):
                with eng.Fori(SECTION * v, SECTION * (v + 1) - 1, 2) as t:
                    body(t, v, False, 0)
                    body(t + 1, v, False, 1)

        def second_loads(t, v, p):
            return loads_before(v) + (v + 1) * (t - SECTION * v) + p // SLOTS

        @block.sync
        def _(sp):
            for dst, src in ((wi, w_item_t), (wu, w_user_t), (wo, w_out_t), (bu, b_user)):
                sp.dma_start(dst[:, :], src).then_inc(consts_in, 16)
            sp.dma_start(b_rows[:, 0:CHUNKS * F], b_item4).then_inc(consts_in, 16)
            sp.dma_start(b_rows[:, CHUNKS * F:], b_out4).then_inc(consts_in, 16)

            def pass1(b, section, first):
                for p, g in enumerate(column_blocks(section)):
                    if not (first and p < SLOTS):
                        sp.wait_ge(pe_groups, BLOCKS * b + p - SLOTS + 1)
                        wait_alone(sp, row_sums, BLOCKS * b + p - SLOTS + 1, waits_passed)
                    sp.dma_start(adj_sb[p % SLOTS][:, :], adj_t[b, g]).then_inc(adj_in[p % SLOTS], 16)

            def pass2(t, v, first, half):
                for p in range(SECTION * (v + 1)):
                    g = BLOCKS - SECTION * (v + 1) + p
                    n = SLOTS * second_loads(t, v, p) + p % SLOTS
                    wait_alone(sp, pe_groups, n - SLOTS + 1, waits_passed)
                    if first:
                        sp.wait_ge(row_sums, BLOCKS * BLOCKS - SLOTS + 1 + p)
                    sp.dma_start(adj_sb[p % SLOTS][:, :], adj_t[BLOCKS - 1 - t, g]).then_inc(adj_in[p % SLOTS], 16)

            first_pass(sp, pass1)
            second_pass(sp, pass2)

        @block.gpsimd
        def _(pool):
            for name in ("u_rstd", "l2_rstd", "deg_pow"):
                pool.sem_inc(S[name], 1)
            pool.memset(ident[:, :], 0.0).then_inc(ident_zero, 1)
            pool.memset(ones_col[:, :], 1.0).then_inc(consts_set, 1)
            pool.memset(ones_row[:, :], 1.0).then_inc(consts_set, 1)
            pool.memset(minus_half[:, :], -0.5).then_inc(consts_set, 1)
            pool.wait_ge(ident_zero, 1)
            pool.affine_select(out=ident[:, :], in_=ident[:, :], compare_op=ALU.not_equal, fill=1.0, base=0,
                               pattern=[[-1, 128]], channel_multiplier=1).then_inc(consts_set, 1)
            for i in range(2):
                pool.dma_start(item_sb[i][:, :], item_t[i]).then_inc(item_in[i], 16)
            with pool.Fori(2, BLOCKS - 1, 2) as i:
                for k in range(2):
                    wait_alone(pool, h_mm, i + k - 1, waits_passed)
                    pool.dma_start(item_sb[k][:, :], item_t[i + k]).then_inc(item_in[k], 16)
            pool.wait_ge(consts_set, 4)

            def power(dst, src, wait_on, signal, k):
                pool.wait_ge(S[wait_on], done(k + 1))
                pool.tensor_tensor(dst[:, :], src[:, :], minus_half[:, :], ALU.pow).then_inc(S[signal], 1)

            def load_x(dst, src, free, signal, k):
                wait_alone(pool, S[free], done(k), waits_passed)
                pool.dma_start(dst[:, :, :].rearrange("p c f -> p (c f)"), src).then_inc(S[signal], 16)

            def end_of_block(e):
                power(dpow, deg1, "deg_safe", "deg_pow", e)
                power(rstd["2"], var["2"], "l2_var", "l2_rstd", e)

            def pass1(b, section, first):
                load_x(xu, x[b], "u_norm", "xu_in", b)
                if not first:
                    load_x(xr, x[b - 1], "x1_made", "xr_in", b - 1)
                power(rstd["u"], var["u"], "u_var", "u_rstd", b)
                if not first:
                    end_of_block(b - 1)

            def pass2(t, v, first, half):
                if first:
                    load_x(xr, x[BLOCKS - 1], "x1_made", "xr_in", BLOCKS - 1)
                    end_of_block(BLOCKS - 1)
                    pool.wait_ge(S["x1_stored"], stored(BLOCKS))
                    wait_alone(pool, S["part_stored"], stored(BLOCKS - SECTION), waits_passed)
                    wait_alone(pool, S["l2_aggr"], done(BLOCKS), waits_passed)
                    wait_alone(pool, S["h2_norm"], done(BLOCKS), waits_passed)
                if v < SECTIONS - 1:
                    wait_alone(pool, S["zt_made"], done(t), waits_passed)
                    pool.dma_start(part[:, :], part_dram[BLOCKS - 1 - t]).then_inc(S["part_in"], 16)
                load_x(x1, x1_dram[BLOCKS - 1 - t], "out_made", "x1_in", t)

            first_pass(pool, pass1)
            second_pass(pool, pass2)

        @block.scalar
        def _(act):
            for name in ("u_relu", "r_relu", "h2_relu", "part_made"):
                act.sem_inc(S[name], 1)
            for name in ("part_stored", "x1_stored", "out_stored"):
                act.sem_inc(S[name], 16)
            act.wait_ge(consts_in, 96)

            def end_of_block(e):
                act.wait_ge(S["x1_made"], done(e + 1))
                act.dma_start(x1_dram[e], x1[:, :, :].rearrange("p c f -> p (c f)")).then_inc(S["x1_stored"], 16)
                act.wait_ge(S["h2_turned"], done(e + 1))
                act.wait_ge(S["sup_mm"], done(e))
                act.activation(h2_t[:, :], ps_h[:, 0:BLOCK], ACT.Relu).then_inc(S["h2_relu"], 1)

            def pass1(b, section, first):
                act.wait_ge(S["u_turned"], done(b + 1))
                act.wait_ge(S["u_added"], done(b))
                act.activation(u_t[:, :], ps_u[:, 0:BLOCK], ACT.Relu).then_inc(S["u_relu"], 1)
                if not first:
                    end_of_block(b - 1)
                if section:
                    act.wait_ge(S["z1_summed"], done(b - SECTION + 1))
                else:
                    act.wait_ge(pe_groups, BLOCKS * (b + 1))
                act.wait_ge(S["r_turned"], done(b))
                act.activation(r_t[:, :], z1[:, 0:BLOCK], ACT.Relu, bias=bu[:, 0:1]).then_inc(S["r_relu"], 1)
                if section:
                    k = b - SECTION
                    act.wait_ge(pe_groups, BLOCKS * (b + 1))
                    act.wait_ge(S["part_stored"], stored(k))
                    act.activation(part[:, :], z2[:, 0:BLOCK], ACT.Copy).then_inc(S["part_made"], 1)
                    act.wait_ge(S["part_made"], done(k + 1))
                    act.dma_start(part_dram[b], part[:, :]).then_inc(S["part_stored"], 16)

            def store_out(t):
                act.wait_ge(S["out_made"], done(t + 1))
                act.dma_start(out[BLOCKS - 1 - t], sup[:, :, :].rearrange("p c f -> p (c f)")).then_inc(
                    S["out_stored"], 16)

            first_pass(act, pass1)
            end_of_block(BLOCKS - 1)
            with act.Fori(0, BLOCKS) as t:
                store_out(t)
            act.wait_ge(S["out_stored"], stored(BLOCKS))

        @block.vector
        def _(dve):
            for name in ("u_stats", "u_aggr", "u_var", "u_norm", "x1_made", "l2_stats", "l2_aggr", "l2_var",
                         "h2_norm", "sup_bias", "s_made", "fold_half", "fold_made", "deg_zero", "deg_safe",
                         "d_cur", "d_made", "zt_made", "zs_added", "out_made"):
                dve.sem_inc(S[name], 1)
            dve.wait_ge(bias_mm, 2)
            dve.tensor_copy(bi_all[:, :], ps_u[0:ROWS, :]).then_inc(bias_done, 1)
            dve.tensor_copy(bo_all[:, :], ps_h[0:ROWS, :]).then_inc(bias_done, 1)
            dve.wait_ge(bias_done, 2)
            with dve.Fori(0, BLOCKS - 1, 2) as i:
                for k, ps in enumerate((ps_s, ps_r)):
                    wait_alone(dve, h_mm, i + k + 1, waits_passed)
                    dve.tensor_tensor(h_sb[:, bass.ts(i + k, CHUNKS * F)], ps[0:ROWS, :], bi_all[:, :],
                                      ALU.add).then_inc(h_done, 1)

            def ln_stats(src, key, n):
                for c in range(CHUNKS):
                    last = dve.bn_stats(stats[key][:, c, :], src[:, c, :])
                return last

            def ln_start(src, key, prefix, k):
                ln_stats(src, key, k).then_inc(S[prefix + "_stats"], 1)
                wait_alone(dve, S[prefix + "_stats"], done(k + 1), waits_passed)
                for c in range(CHUNKS):
                    last = dve.bn_aggr(mv[key][:, c, :], stats[key][:, c, :])
                last.then_inc(S[prefix + "_aggr"], 1)
                dve.wait_ge(S[prefix + "_aggr"], done(k + 1))
                dve.tensor_scalar(var[key][:, :], mv[key][:, :, 1], LN_EPS, None, ALU.add).then_inc(
                    S[prefix + "_var"], 1)

            def ln_apply(dst, src, key, prefix, k, signal):
                dve.wait_ge(S[prefix + "_rstd"], done(k + 1))
                for c in range(CHUNKS):
                    last = dve.tensor_scalar(dst[:, c, :], src[:, c, :], mv[key][:, c, 0:1], rstd[key][:, c:c + 1],
                                             ALU.subtract, ALU.mult)
                last.then_inc(S[signal], 1)

            def degrees(e):
                dve.wait_ge(S["deg_mm"], done(e + 1))
                dve.tensor_scalar(deg0[:, :], ps_d[0:ROWS, 0:CHUNKS], 1.0, 0.0, ALU.add, ALU.is_equal).then_inc(
                    S["deg_zero"], 1)
                dve.wait_ge(S["deg_zero"], done(e + 1))
                dve.scalar_tensor_tensor(out=deg1[:, :], in0=ps_d[0:ROWS, 0:CHUNKS], scalar=1.0, in1=deg0[:, :],
                                         op0=ALU.add, op1=ALU.add).then_inc(S["deg_safe"], 1)

            def scales(e):
                dve.wait_ge(S["deg_pow"], done(e + 1))
                dve.tensor_tensor(dcur[:, :], dpow[:, :], deg0[:, :], ALU.subtract).then_inc(S["d_cur"], 1)
                wait_alone(dve, S["d_cur"], done(e + 1), waits_passed)
                dve.tensor_copy(d_sb[:, bass.ts(e, CHUNKS)], dcur[:, :]).then_inc(S["d_made"], 1)

            def first_residual(e):
                dve.wait_ge(S["r_turned"], done(e + 1))
                dve.wait_ge(S["xr_in"], loaded(e + 1))
                dve.wait_ge(S["x1_stored"], stored(e))
                dve.tensor_tensor(x1[:, :, :].rearrange("p c f -> p (c f)"), ps_r[0:ROWS, :],
                                  xr[:, :, :].rearrange("p c f -> p (c f)"), ALU.add).then_inc(S["x1_made"], 1)
                dve.wait_ge(S["x1_made"], done(e + 1))
                ln_start(x1, "2", "l2", e)

            def second_norm(e):
                dve.wait_ge(S["h2_turned"], done(e))
                ln_apply(h2, x1, "2", "l2", e, "h2_norm")

            def second_features(e):
                dve.wait_ge(S["sup_mm"], done(e + 1))
                dve.tensor_tensor(sup[:, :, :].rearrange("p c f -> p (c f)"), ps_s[0:ROWS, :], bo_all[:, :],
                                  ALU.add).then_inc(S["sup_bias"], 1)
                wait_alone(dve, S["sup_bias"], done(e + 1), waits_passed)
                s_e = s_sb[:, bass.ts(e, CHUNKS * F)].rearrange("p (c f) -> p c f", c=CHUNKS)
                for c in range(CHUNKS):
                    last = dve.tensor_scalar(s_e[:, c, :], sup[:, c, :], dcur[:, c:c + 1], None, ALU.mult)
                last.then_inc(S["s_made"], 1)

            def pass1(b, section, first):
                for p in range(BLOCKS):
                    if p == 2:
                        dve.wait_ge(S["xu_in"], loaded(b + 1))
                        ln_start(xu, "u", "u", b)
                    if p == 3:
                        dve.wait_ge(S["u_turned"], done(b))
                        ln_apply(xn, xu, "u", "u", b, "u_norm")
                    if not first:
                        if p == 4:
                            degrees(b - 1)
                        if p == 6:
                            scales(b - 1)
                        if p == 8:
                            first_residual(b - 1)
                        if p == 10:
                            second_norm(b - 1)
                        if p == 14:
                            second_features(b - 1)
                    dve.wait_ge(adj_in[p % SLOTS], 16 * (PER_SLOT * b + p // SLOTS + 1))
                    if p == 1:
                        if not first:
                            dve.wait_ge(S["fold_made"], done(b))
                        dve.tensor_tensor(acc[:, :], adj_sb[0][0:ROWS, :], adj_sb[1][0:ROWS, :], ALU.add).then_inc(
                            row_sums, 2)
                    if p > 1:
                        dve.wait_ge(row_sums, BLOCKS * b + p)
                        dve.tensor_tensor(acc[:, :], acc[:, :], adj_sb[p % SLOTS][0:ROWS, :], ALU.add).then_inc(
                            row_sums, 1)
                half = GROUP // 2
                dve.wait_ge(row_sums, BLOCKS * (b + 1))
                dve.tensor_tensor(acc[:, 0:half], acc[:, 0:half], acc[:, half:], ALU.add).then_inc(S["fold_half"], 1)
                dve.wait_ge(S["fold_half"], done(b + 1))
                dve.wait_ge(S["deg_mm"], done(b))
                dve.tensor_tensor(fold[:, :], acc[:, 0:BLOCK], acc[:, BLOCK:half], ALU.add).then_inc(
                    S["fold_made"], 1)

            def take_sum(t, v, half):
                dve.wait_ge(pe_groups, SLOTS * second_loads(t + 1, v, 0))
                dve.wait_ge(S["zt_turned"], done(t))
                if v < SECTIONS - 1:
                    dve.wait_ge(S["part_in"], loaded(t + 1))
                    dve.tensor_tensor(r_t[:, :], z_banks[half][:, 0:BLOCK], part[:, :], ALU.add).then_inc(
                        S["zt_made"], 1)
                else:
                    dve.tensor_copy(r_t[:, :], z_banks[half][:, 0:BLOCK]).then_inc(S["zt_made"], 1)

            def finish(t):
                dve.wait_ge(S["zt_turned"], done(t + 1))
                wait_alone(dve, S["out_stored"], stored(t), waits_passed)
                s_b = s_sb[:, bass.ts(BLOCKS - 1 - t, CHUNKS * F)]
                dve.tensor_tensor(h2[:, :, :].rearrange("p c f -> p (c f)"), ps_r[0:ROWS, :], s_b, ALU.add).then_inc(
                    S["zs_added"], 1)
                dve.tensor_copy(dcur[:, :], d_sb[:, bass.ts(BLOCKS - 1 - t, CHUNKS)]).then_inc(S["d_cur"], 1)
                dve.wait_ge(S["zs_added"], done(t + 1))
                dve.wait_ge(S["d_cur"], done(BLOCKS + t + 1))
                dve.wait_ge(S["x1_in"], loaded(t + 1))
                for c in range(CHUNKS):
                    last = dve.scalar_tensor_tensor(out=sup[:, c, :], in0=h2[:, c, :], scalar=dcur[:, c:c + 1],
                                                    in1=x1[:, c, :], op0=ALU.mult, op1=ALU.add)
                last.then_inc(S["out_made"], 1)

            def pass2(t, v, first, half):
                if first:
                    degrees(BLOCKS - 1)
                    first_residual(BLOCKS - 1)
                    scales(BLOCKS - 1)
                    second_norm(BLOCKS - 1)
                    second_features(BLOCKS - 1)
                else:
                    finish(t - 1)
                take_sum(t, v, half)

            first_pass(dve, pass1)
            second_pass(dve, pass2)
            finish(BLOCKS - 1)

        @block.tensor
        def _(pe):
            for name in ("u_turned", "u_added", "z1_summed", "r_turned", "h2_turned", "sup_mm", "deg_mm",
                         "zt_turned"):
                pe.sem_inc(S[name], 1)
            pe.wait_ge(consts_in, 96)
            pe.wait_ge(consts_set, 4)
            for i, ps in enumerate((ps_u, ps_h)):
                pe.matmul(ps[0:ROWS, :], ones_row[:, 0:ROWS], b_rows[:, CHUNKS * F * i:CHUNKS * F * (i + 1)],
                          start=True, stop=True).then_inc(bias_mm, 1)
            def item_block(i, k, ps):
                for c in range(CHUNKS):
                    last = pe.matmul(ps[0:ROWS, c * F:(c + 1) * F], item_sb[k][:, c * ROWS:(c + 1) * ROWS], wi[:, :],
                                     start=True, stop=True)
                last.then_inc(h_mm, 1)

            for k, ps in enumerate((ps_s, ps_r)):
                pe.wait_ge(item_in[k], 16)
                item_block(k, k, ps)
            with pe.Fori(2, BLOCKS - 1, 2) as i:
                for k, ps in enumerate((ps_s, ps_r)):
                    pe.wait_ge(h_done, i + k - 1)
                    pe.wait_ge(item_in[k], 8 * i + 16)
                    item_block(i + k, k, ps)
            pe.wait_ge(h_done, BLOCKS)

            def features(src, g, c):
                at = (g * CHUNKS + c) * F
                return src[:, at:at + F]

            def adj_chunk(p, c):
                return adj_sb[p % SLOTS][0:ROWS, c * BLOCK:(c + 1) * BLOCK]

            def turn_rows(ps, src, signal):
                for c in range(CHUNKS):
                    last = pe.transpose(ps[:, c * ROWS:(c + 1) * ROWS], src[:, c, :], ident[0:ROWS, 0:ROWS])
                last.then_inc(S[signal], 1)

            def turn_back(ps, src, signal):
                for c in range(CHUNKS):
                    last = pe.transpose(ps[0:ROWS, c * F:(c + 1) * F], src[:, c * ROWS:(c + 1) * ROWS], ident[:, :])
                last.then_inc(S[signal], 1)

            def degree_sums(e):
                pe.wait_ge(S["fold_made"], done(e + 1))
                pe.wait_ge(S["deg_safe"], done(e))
                for c in range(CHUNKS):
                    last = pe.matmul(ps_d[0:ROWS, c:c + 1], fold[:, c * ROWS:(c + 1) * ROWS], ones_col[0:ROWS, :],
                                     start=True, stop=True)
                last.then_inc(S["deg_mm"], 1)

            def turn_r(e):
                pe.wait_ge(S["r_relu"], done(e + 1))
                pe.wait_ge(S["x1_made"], done(e))
                turn_back(ps_r, r_t, "r_turned")

            def turn_h2(e):
                pe.wait_ge(S["h2_norm"], done(e + 1))
                pe.wait_ge(S["h2_relu"], done(e))
                turn_rows(ps_h, h2, "h2_turned")

            def support(e):
                pe.wait_ge(S["h2_relu"], done(e + 1))
                pe.wait_ge(S["s_made"], done(e))
                for c in range(CHUNKS):
                    last = pe.matmul(ps_s[0:ROWS, c * F:(c + 1) * F], h2_t[:, c * ROWS:(c + 1) * ROWS], wo[:, :],
                                     start=True, stop=True)
                last.then_inc(S["sup_mm"], 1)

            def pass1(b, section, first):
                order = column_blocks(section)
                known = BLOCKS - SECTION * section
                if not first:
                    degree_sums(b - 1)
                    pe.wait_ge(S["r_relu"], done(b))
                for p, g in enumerate(order):
                    pe.wait_ge(adj_in[p % SLOTS], 16 * (PER_SLOT * b + p // SLOTS + 1))
                    for c in range(CHUNKS):
                        ends = p == BLOCKS - 1 and c == CHUNKS - 1
                        last = pe.matmul(z1[:, 0:BLOCK], features(h_sb, g, c), adj_chunk(p, c),
                                         start=(p == 0 and c == 0), stop=ends)
                        if ends and section:
                            last.then_inc(S["z1_summed"], 1)
                        elif c == CHUNKS - 1 and p < known:
                            last.then_inc(pe_groups, 1)
                    if p >= known:
                        if p == known:
                            pe.wait_ge(S["part_made"], done(b - SECTION))
                            pe.wait_ge(S["s_made"], done(SECTION * section - 1))
                        if p == BLOCKS - 1:
                            pe.wait_ge(S["s_made"], done(SECTION * section))
                        for c in range(CHUNKS):
                            last = pe.matmul(z2[:, 0:BLOCK], features(s_sb, g, c), adj_chunk(p, c),
                                             start=(p == known and c == 0), stop=(p == BLOCKS - 1 and c == CHUNKS - 1))
                        last.then_inc(pe_groups, 1)
                    if p == 4:
                        pe.wait_ge(S["u_norm"], done(b + 1))
                        pe.wait_ge(S["u_relu"], done(b))
                        turn_rows(ps_u, xn, "u_turned")
                    if p == 6:
                        pe.wait_ge(S["u_relu"], done(b + 1))
                        pe.matmul(z1[:, 0:BLOCK], wu[:, :], u_t[:, :], start=False, stop=False).then_inc(
                            S["u_added"], 1)
                    if not first:
                        if p == 5:
                            turn_r(b - 1)
                        if p == 10:
                            turn_h2(b - 1)
                        if p == 12:
                            support(b - 1)

            def pass2(t, v, first, half):
                n = SECTION * (v + 1)
                z = z_banks[half]
                if first:
                    degree_sums(BLOCKS - 1)
                    pe.wait_ge(S["r_relu"], done(BLOCKS))
                    pe.wait_ge(S["part_made"], done(BLOCKS - SECTION))
                elif not (v == 0 and isinstance(t, int) and t < 2):
                    pe.wait_ge(S["zt_made"], done(t - 1))
                for p in range(n):
                    g = BLOCKS - n + p
                    pe.wait_ge(adj_in[p % SLOTS], 16 * (second_loads(t, v, p) + 1))
                    if first and p == n - 1:
                        support(BLOCKS - 1)
                        pe.wait_ge(S["s_made"], done(BLOCKS))
                    for c in range(CHUNKS):
                        ends = p == n - 1 and c == CHUNKS - 1
                        last = pe.matmul(z[:, 0:BLOCK], features(s_sb, g, c), adj_chunk(p, c),
                                         start=(p == 0 and c == 0), stop=ends)
                    last.then_inc(pe_groups, 1)
                    if first and p == 0:
                        turn_r(BLOCKS - 1)
                    if first and p == 1:
                        turn_h2(BLOCKS - 1)
                    if not first and p == 1:
                        turn_sum(t - 1)

            def turn_sum(t):
                pe.wait_ge(S["zt_made"], done(t + 1))
                pe.wait_ge(S["out_made"], done(t))
                turn_back(ps_r, r_t, "zt_turned")

            first_pass(pe, pass1)
            second_pass(pe, pass2)
            turn_sum(BLOCKS - 1)


def build(nc, shapes):
    def dram(name, shape, kind="ExternalInput"):
        return nc.dram_tensor(name, shape, F32, kind=kind).ap()

    args = [dram(n, s) for n, s in shapes]
    out = dram("out_0_dram", (BLOCKS, ROWS, CHUNKS * F), "ExternalOutput")
    gnn_two_layers(nc, *args, out)


def kernel(x, adj, L0_gnn_item_feat, L0_gnn_W_item, L0_gnn_b_item, L0_gnn_W_user, L0_gnn_b_user, L1_gnn_W, L1_gnn_b):
    import numpy as np
    import concourse.bacc as bacc
    from concourse.bass_utils import run_bass_kernel_spmd

    def by_chunks(a):
        return np.ascontiguousarray(a.reshape(BLOCKS, CHUNKS, ROWS, F).transpose(0, 2, 1, 3)).reshape(
            BLOCKS, ROWS, CHUNKS * F)

    adj = np.asarray(adj)
    adj_t = np.zeros((BLOCKS, BLOCKS, 128, CHUNKS, BLOCK), adj.dtype)
    adj_t[:, :, :ROWS] = adj.reshape(BLOCKS, BLOCK, BLOCKS, CHUNKS, ROWS).transpose(0, 2, 4, 3, 1)
    arrays = {
        "in_x": by_chunks(np.asarray(x)),
        "in_adj_t": adj_t.reshape(BLOCKS, BLOCKS, 128, GROUP),
        "in_item_t": np.ascontiguousarray(np.asarray(L0_gnn_item_feat).reshape(BLOCKS, BLOCK, F).transpose(0, 2, 1)),
        "in_w_item_t": np.ascontiguousarray(np.asarray(L0_gnn_W_item).T),
        "in_b_item": np.tile(np.asarray(L0_gnn_b_item), CHUNKS).reshape(1, CHUNKS * F),
        "in_w_user_t": np.ascontiguousarray(np.asarray(L0_gnn_W_user).T),
        "in_b_user": np.asarray(L0_gnn_b_user).reshape(F, 1),
        "in_w_out_t": np.ascontiguousarray(np.asarray(L1_gnn_W).T),
        "in_b_out": np.tile(np.asarray(L1_gnn_b), CHUNKS).reshape(1, CHUNKS * F),
    }
    nc = bacc.Bacc("TRN2", target_bir_lowering=False, num_devices=1)
    build(nc, [(n, a.shape) for n, a in arrays.items()])
    r = run_bass_kernel_spmd(nc, [arrays], core_ids=[0])
    got = r.results[0]["out_0_dram"]
    return got.reshape(BLOCKS, ROWS, CHUNKS, F).transpose(0, 2, 1, 3).reshape(N, F)
```

```python
import concourse.bass as bass
from concourse import mybir
from contextlib import ExitStack

F32 = mybir.dt.float32
F32R = mybir.dt.float32r
ALU = mybir.AluOpType
ACT = mybir.ActivationFunctionType

N = 10000
F = 128
ROWS = 125
CHUNKS = 4
BLOCK = ROWS * CHUNKS
BLOCKS = N // BLOCK
GROUP = CHUNKS * BLOCK
SECTION = 4
SECTIONS = BLOCKS // SECTION
SLOTS = 4
PER_SLOT = BLOCKS // SLOTS
SPLIT = 8
NATIVE = BLOCKS - SPLIT
HALF = GROUP // 2
RING = 4
LN_EPS = 1e-5


def done(n):
    return n + 1


def stored(n):
    return 16 * (n + 1)


def loaded(n):
    return 16 * n


def wait_alone(eng, semaphore, value, passed):
    eng.wait_ge(semaphore, value)
    eng.sem_inc(passed, 1)


def is_split(g):
    return g < SPLIT


def column_blocks(section):
    known = SECTION * section
    last = [known - 1] if section else []
    natives = [g for g in list(range(known, BLOCKS)) + list(range(known - 1)) if not is_split(g)]
    splits = [g for g in list(range(known, BLOCKS)) + list(range(known)) if is_split(g)]
    natives = [g for g in natives if g not in last]
    splits = [g for g in splits if g not in last]
    return natives[:2] + spread(natives[2:], splits) + last


def spread(few, many):
    return [g for _, _, g in sorted([((i + 0.5) / len(few), 0, g) for i, g in enumerate(few)]
                                    + [((i + 0.5) / len(many), 1, g) for i, g in enumerate(many)])]


HELD = BLOCKS - SPLIT


def second_split(v, g):
    return v > 0 and (is_split(g) or g >= HELD)


def second_blocks(v):
    blocks = range(BLOCKS - SECTION * (v + 1), BLOCKS)
    natives = [g for g in blocks if not second_split(v, g)]
    splits = [g for g in blocks if second_split(v, g)]
    if not splits:
        return natives
    out = [g for pair in zip(natives, splits) for g in pair]
    return out + splits[len(natives):]


def splits_in(v):
    return sum(second_split(v, g) for g in second_blocks(v))


def halves_before(t, v):
    return 2 * (SPLIT * BLOCKS + SECTION * sum(splits_in(u) for u in range(v)) + splits_in(v) * (t - SECTION * v))


def natives_before(t, v):
    natives = [SECTION * (u + 1) - splits_in(u) for u in range(v + 1)]
    return NATIVE * BLOCKS + SECTION * sum(natives[:v]) + natives[v] * (t - SECTION * v)


def loads_before(section_index):
    return PER_SLOT * BLOCKS + SECTION * section_index * (section_index + 1) // 2


def gnn_two_layers(nc, x, adj_t, item_t, w_item_t, b_item4, w_user_t, b_user, w_out_t, b_out4, out):
    ctx = ExitStack()
    with ctx:
        def sb(name, shape, dt=F32):
            return ctx.enter_context(nc.sbuf_tensor(name, shape, dt))

        def bank(name):
            return ctx.enter_context(nc.psum_tensor(name, [128, 512], F32))

        def sem(name):
            return ctx.enter_context(nc.semaphore(name))

        x1_dram = nc.dram_tensor("x1_dram", (BLOCKS, ROWS, CHUNKS * F), F32, kind="Internal").ap()
        part_dram = nc.dram_tensor("part_dram", (BLOCKS, F, BLOCK), F32, kind="Internal").ap()

        h_high = sb("h_high", [ROWS, SPLIT * CHUNKS * F], F32R)
        h_low = sb("h_low", [ROWS, SPLIT * CHUNKS * F], F32R)
        h_whole = sb("h_whole", [ROWS, NATIVE * CHUNKS * F])
        s_high = sb("s_high", [ROWS, SPLIT * CHUNKS * F], F32R)
        s_low = sb("s_low", [ROWS, SPLIT * CHUNKS * F], F32R)
        s_whole = sb("s_whole", [ROWS, NATIVE * CHUNKS * F])
        adj_high = [sb(f"adj_high{i}", [ROWS, HALF], F32R) for i in range(RING)]
        adj_low = [sb(f"adj_low{i}", [ROWS, HALF], F32R) for i in range(RING)]
        d_sb = sb("d_sb", [ROWS, BLOCKS * CHUNKS])
        adj_sb = [sb(f"adj{i}", [128, GROUP]) for i in range(SLOTS)]
        acc = sb("acc", [ROWS, GROUP])
        fold = sb("fold", [128, BLOCK])

        ident = sb("ident", [128, 128])
        ones_col = sb("ones_col", [128, 1])
        ones_row = sb("ones_row", [1, 128])
        minus_half = sb("minus_half", [ROWS, CHUNKS])
        wu = sb("wu", [F, F])
        wo = sb("wo", [F, F])
        bu = sb("bu", [F, 1])
        bo_all = sb("bo_all", [ROWS, CHUNKS * F])

        x_in = sb("x_in", [ROWS, CHUNKS, F])
        normed = sb("normed", [ROWS, CHUNKS, F])
        x1 = sb("x1", [ROWS, CHUNKS, F])
        turned = sb("turned", [F, BLOCK])
        r_t = sb("r_t", [F, BLOCK])
        part = sb("part", [F, BLOCK])
        w_item = fold[:, 0:F]
        item_sb = [r_t, turned]
        bi_all = x1[:, :, :].rearrange("p c f -> p (c f)")
        h_tmp = [normed[:, :, :].rearrange("p c f -> p (c f)"), x_in[:, :, :].rearrange("p c f -> p (c f)")]
        b_item_row, b_out_row = h_tmp[0][0:1, :], h_tmp[1][0:1, :]
        stats = {k: sb(f"stats_{k}", [ROWS, CHUNKS, 6]) for k in "u2"}
        mv = {k: sb(f"mv_{k}", [ROWS, CHUNKS, 2]) for k in "u2"}
        var = {k: sb(f"var_{k}", [ROWS, CHUNKS]) for k in "u2"}
        rstd = {k: sb(f"rstd_{k}", [ROWS, CHUNKS]) for k in "u2"}
        deg0 = sb("deg0", [ROWS, CHUNKS])
        deg1 = sb("deg1", [ROWS, CHUNKS])
        dpow = sb("dpow", [ROWS, CHUNKS])
        dcur = sb("dcur", [ROWS, CHUNKS])

        z1, z2, ps_u, ps_r, ps_h, ps_s, ps_d = (bank(n) for n in ("z1", "z2", "ps_u", "ps_r", "ps_h", "ps_s", "ps_d"))
        z_banks = [z1, z2]

        consts_in = sem("consts_in")
        consts_set = sem("consts_set")
        ident_zero = sem("ident_zero")
        item_in = [sem(f"item_in{i}") for i in range(2)]
        bias_mm = sem("bias_mm")
        bias_done = sem("bias_done")
        h_mm = sem("h_mm")
        h_done = sem("h_done")
        adj_in = [sem(f"adj_in{i}") for i in range(SLOTS)]
        highs_made = sem("highs_made")
        lows_made = sem("lows_made")
        halves_used = sem("halves_used")
        natives_used = sem("natives_used")
        row_sums = sem("row_sums")
        waits_passed = sem("waits_passed")

        STAGES = ("u_stats", "u_aggr", "u_var", "u_rstd", "u_norm", "u_turned", "u_relu", "u_added",
                  "z1_summed", "r_relu", "r_turned", "x1_made", "l2_stats", "l2_aggr", "l2_var", "l2_rstd",
                  "h2_norm", "h2_turned", "h2_relu", "sup_mm", "sup_bias", "s_scaled", "s_high", "s_made",
                  "x1s_made",
                  "fold_half", "fold_made", "deg_mm", "deg_zero", "deg_safe", "deg_pow", "d_cur", "d_made",
                  "part_made", "zt_made", "zt_turned", "out_made")
        STAGES_DMA = ("xu_in", "xr_in", "x1_stored", "part_stored", "part_in", "x1_in", "out_stored")
        S = {n: sem(n) for n in STAGES + STAGES_DMA}
        part_zero = sem("part_zero")
        h_sum = sem("h_sum")
        h_high_made = sem("h_high_made")
        held_high = sem("held_high")
        held_low = sem("held_low")

        block = ctx.enter_context(nc.Block())

        def first_pass(eng, body):
            for lo, hi in ((0, 1), (1, 4), (4, 8), (8, 9), (9, 12), (12, 16), (16, 20)):
                if hi - lo == 1:
                    body(lo, lo // SECTION, lo == 0)
                else:
                    with eng.Fori(lo, hi) as b:
                        body(b, lo // SECTION, False)

        def before_is_split(b, section):
            return b <= SPLIT if isinstance(b, int) else section < SPLIT // SECTION

        def second_pass(eng, body):
            for t in range(SECTION):
                body(t, 0, t == 0, t % 2)
            for v in range(1, SECTIONS):
                with eng.Fori(SECTION * v, SECTION * (v + 1) - 1, 2) as t:
                    body(t, v, False, 0)
                    body(t + 1, v, False, 1)

        def whole_block(features, i):
            return features[:, i * CHUNKS * F:(i + 1) * CHUNKS * F]

        def second_loads(t, v, p):
            return loads_before(v) + (v + 1) * (t - SECTION * v) + p // SLOTS

        @block.sync
        def _(sp):
            for dst, src in ((w_item, w_item_t), (wu[:, :], w_user_t), (wo[:, :], w_out_t), (bu[:, :], b_user),
                             (b_item_row, b_item4), (b_out_row, b_out4)):
                sp.dma_start(dst, src).then_inc(consts_in, 16)

            def natives_up_to(section, p):
                return sum(not is_split(g) for g in column_blocks(section)[:p + 1])

            def pass1(b, section, first):
                for p, g in enumerate(column_blocks(section)):
                    if not (first and p < SLOTS):
                        wait_alone(sp, row_sums, BLOCKS * b + p - SLOTS + 1, waits_passed)
                        if p >= SLOTS:
                            natives = NATIVE * b + natives_up_to(section, p - SLOTS)
                        else:
                            natives = NATIVE * b - min(NATIVE - natives_up_to(q, BLOCKS - SLOTS + p)
                                                       for q in range(SECTIONS))
                        if not first or natives > 0:
                            wait_alone(sp, natives_used, natives, waits_passed)
                    sp.dma_start(adj_sb[p % SLOTS][:, :], adj_t[b, g]).then_inc(adj_in[p % SLOTS], 16)

            def pass2(t, v, first, half):
                order = second_blocks(v)
                for p, g in enumerate(order):
                    if first:
                        sp.wait_ge(row_sums, BLOCKS * BLOCKS - SLOTS + 1 + p)
                        sp.wait_ge(natives_used, NATIVE * (BLOCKS - 1)
                                   + natives_up_to(SECTIONS - 1, BLOCKS - SLOTS + p))
                    elif v == 0:
                        sp.wait_ge(natives_used, natives_before(t - 1, v) + p + 1)
                    else:
                        if p < SLOTS:
                            natives = natives_before(t, v)
                            halves = halves_before(t, v) - 2 * (SLOTS - 1 - p)
                        else:
                            natives = natives_before(t, v) + sum(not second_split(v, q) for q in order[:p - SLOTS + 1])
                            halves = halves_before(t, v) + 2 * sum(second_split(v, q) for q in order[:p - SLOTS + 1])
                        wait_alone(sp, natives_used, natives, waits_passed)
                        wait_alone(sp, lows_made, halves, waits_passed)
                    sp.dma_start(adj_sb[p % SLOTS][:, :], adj_t[BLOCKS - 1 - t, g]).then_inc(adj_in[p % SLOTS], 16)

            first_pass(sp, pass1)
            second_pass(sp, pass2)

        @block.gpsimd
        def _(pool):
            for name in ("u_rstd", "l2_rstd", "deg_pow"):
                pool.sem_inc(S[name], 1)
            pool.memset(ident[:, :], 0.0).then_inc(ident_zero, 1)
            pool.memset(ones_col[:, :], 1.0).then_inc(consts_set, 1)
            pool.memset(ones_row[:, :], 1.0).then_inc(consts_set, 1)
            pool.memset(minus_half[:, :], -0.5).then_inc(consts_set, 1)
            pool.wait_ge(ident_zero, 1)
            pool.affine_select(out=ident[:, :], in_=ident[:, :], compare_op=ALU.not_equal, fill=1.0, base=0,
                               pattern=[[-1, 128]], channel_multiplier=1).then_inc(consts_set, 1)
            for i in range(2):
                pool.dma_start(item_sb[i][:, :], item_t[i]).then_inc(item_in[i], 16)
            with pool.Fori(2, BLOCKS - 1, 2) as i:
                for k in range(2):
                    wait_alone(pool, h_mm, i + k - 1, waits_passed)
                    pool.dma_start(item_sb[k][:, :], item_t[i + k]).then_inc(item_in[k], 16)
            pool.wait_ge(consts_set, 4)

            def power(dst, src, wait_on, signal, k):
                pool.wait_ge(S[wait_on], done(k + 1))
                pool.tensor_tensor(dst[:, :], src[:, :], minus_half[:, :], ALU.pow).then_inc(S[signal], 1)

            def load_x(dst, src, signal):
                pool.dma_start(dst[:, :, :].rearrange("p c f -> p (c f)"), src).then_inc(S[signal], 16)

            def end_of_block(e):
                load_x(x_in, x[e], "xr_in")
                power(dpow, deg1, "deg_safe", "deg_pow", e)
                power(rstd["2"], var["2"], "l2_var", "l2_rstd", e)

            def pass1(b, section, first):
                if first:
                    pool.wait_ge(h_high_made, SPLIT)
                    pool.wait_ge(h_done, BLOCKS)
                else:
                    wait_alone(pool, S["u_norm"], done(b), waits_passed)
                    wait_alone(pool, S["x1_made"], done(b - 1), waits_passed)
                load_x(x_in, x[b], "xu_in")
                power(rstd["u"], var["u"], "u_var", "u_rstd", b)
                if not first:
                    wait_alone(pool, S["u_norm"], done(b + 1), waits_passed)
                    end_of_block(b - 1)

            def pass2(t, v, first, half):
                if first:
                    wait_alone(pool, S["x1_made"], done(BLOCKS - 1), waits_passed)
                    end_of_block(BLOCKS - 1)
                    pool.wait_ge(S["x1_stored"], stored(BLOCKS))
                    pool.wait_ge(S["part_stored"], loaded(BLOCKS))
                wait_alone(pool, S["zt_made"], done(t), waits_passed)
                pool.dma_start(part[:, :], part_dram[BLOCKS - 1 - t]).then_inc(S["part_in"], 16)
                wait_alone(pool, S["out_made"], done(t), waits_passed)
                load_x(x1, x1_dram[BLOCKS - 1 - t], "x1_in")

            first_pass(pool, pass1)
            second_pass(pool, pass2)

        @block.scalar
        def _(act):
            for name in ("u_relu", "r_relu", "h2_relu", "part_made"):
                act.sem_inc(S[name], 1)
            for name in ("x1_stored", "out_stored"):
                act.sem_inc(S[name], 16)
            act.wait_ge(part_zero, 1)
            for b in range(SECTION):
                act.dma_start(part_dram[b], part[:, :]).then_inc(S["part_stored"], 16)
            act.wait_ge(consts_in, 96)
            with act.Fori(0, SPLIT - 1, 2) as i:
                for k in range(2):
                    act.wait_ge(h_sum, i + k + 1)
                    act.activation(h_high[:, bass.ts(i + k, CHUNKS * F)], h_tmp[k], ACT.Copy).then_inc(h_high_made, 1)

            def round_half(m, ring, p, half):
                if not isinstance(m, int) or m >= RING:
                    act.wait_ge(halves_used, m - RING + 1)
                act.activation(adj_high[ring % RING][:, :], adj_sb[p % SLOTS][0:ROWS, half * HALF:(half + 1) * HALF],
                               ACT.Copy).then_inc(highs_made, 1)

            def store_x1(e):
                act.wait_ge(S["x1s_made"], done(e + 1))
                act.dma_start(x1_dram[e], x1[:, :, :].rearrange("p c f -> p (c f)")).then_inc(S["x1_stored"], 16)

            def relu_h2(e):
                act.wait_ge(S["h2_turned"], done(e + 1))
                act.activation(turned[:, :], ps_h[:, 0:BLOCK], ACT.Relu).then_inc(S["h2_relu"], 1)

            def pass1(b, section, first):
                n = 0
                for p, g in enumerate(column_blocks(section)):
                    if p == 7:
                        act.wait_ge(S["u_turned"], done(b + 1))
                        if not first:
                            act.wait_ge(S["sup_mm"], done(b - 1))
                        act.activation(turned[:, :], ps_u[:, 0:BLOCK], ACT.Relu).then_inc(S["u_relu"], 1)
                    if p == 13 and not first:
                        act.wait_ge(S["u_added"], done(b + 1))
                        relu_h2(b - 1)
                    if p == BLOCKS - 1 and not first:
                        store_x1(b - 1)
                    if is_split(g):
                        act.wait_ge(adj_in[p % SLOTS], 16 * (PER_SLOT * b + p // SLOTS + 1))
                        for half in range(2):
                            round_half(2 * SPLIT * b + n, n, p, half)
                            n += 1
                if section:
                    act.wait_ge(S["z1_summed"], done(b - SECTION + 1))
                else:
                    act.wait_ge(halves_used, 2 * SPLIT * (b + 1))
                    act.wait_ge(natives_used, NATIVE * (b + 1))
                act.wait_ge(S["r_turned"], done(b))
                act.activation(r_t[:, :], z1[:, 0:BLOCK], ACT.Relu, bias=bu[:, 0:1]).then_inc(S["r_relu"], 1)
                if section:
                    act.wait_ge(halves_used, 2 * SPLIT * (b + 1))
                    act.wait_ge(natives_used, NATIVE * (b + 1))
                    act.wait_ge(S["part_stored"], loaded(b))
                    act.activation(part[:, :], z2[:, 0:BLOCK], ACT.Copy).then_inc(S["part_made"], 1)
                    act.wait_ge(S["part_made"], done(b - SECTION + 1))
                    act.dma_start(part_dram[b], part[:, :]).then_inc(S["part_stored"], 16)

            def store_out(t):
                act.wait_ge(S["out_made"], done(t + 1))
                act.dma_start(out[BLOCKS - 1 - t], normed[:, :, :].rearrange("p c f -> p (c f)")).then_inc(
                    S["out_stored"], 16)

            def pass2(t, v, first, half):
                if first:
                    relu_h2(BLOCKS - 1)
                    store_x1(BLOCKS - 1)
                    act.wait_ge(halves_used, 2 * SPLIT * BLOCKS)
                    for g in range(HELD, BLOCKS):
                        act.activation(whole_block(h_high, g - HELD), whole_block(s_whole, g - SPLIT),
                                       ACT.Copy).then_inc(held_high, 1)
                n = 0
                for p, g in enumerate(second_blocks(v)):
                    if p == min(9, SECTION * (v + 1) - 1) and not first:
                        store_out(t - 1)
                    if second_split(v, g):
                        act.wait_ge(adj_in[p % SLOTS], 16 * (second_loads(t, v, p) + 1))
                        for h in range(2):
                            round_half(halves_before(t, v) + n, n, p, h)
                            n += 1

            first_pass(act, pass1)
            second_pass(act, pass2)
            store_out(BLOCKS - 1)
            act.wait_ge(S["out_stored"], stored(BLOCKS))

        @block.vector
        def _(dve):
            for name in ("u_stats", "u_aggr", "u_var", "u_norm", "x1_made", "l2_stats", "l2_aggr", "l2_var",
                         "h2_norm", "sup_bias", "s_scaled", "s_high", "s_made", "x1s_made", "fold_half",
                         "fold_made", "deg_zero", "deg_safe", "d_cur", "d_made", "zt_made", "out_made"):
                dve.sem_inc(S[name], 1)
            dve.memset(part[:, :], 0.0).then_inc(part_zero, 1)
            dve.wait_ge(bias_mm, 2)
            dve.tensor_copy(bi_all, ps_u[0:ROWS, :]).then_inc(bias_done, 1)
            dve.tensor_copy(bo_all[:, :], ps_h[0:ROWS, :]).then_inc(bias_done, 1)
            dve.wait_ge(bias_done, 2)

            def split_h(i, k, ps):
                wait_alone(dve, h_mm, i + k + 1, waits_passed)
                dve.tensor_tensor(h_tmp[k], ps[0:ROWS, :], bi_all, ALU.add).then_inc(h_sum, 1)
                at = bass.ts(i + k, CHUNKS * F)
                wait_alone(dve, h_high_made, i + k + 1, waits_passed)
                dve.tensor_tensor(h_low[:, at], h_tmp[k], h_high[:, at].bitcast(F32), ALU.subtract).then_inc(h_done, 1)

            with dve.Fori(0, SPLIT - 1, 2) as i:
                for k, ps in enumerate((ps_s, ps_r)):
                    split_h(i, k, ps)
            with dve.Fori(SPLIT, BLOCKS - 1, 2) as i:
                for k, ps in enumerate((ps_s, ps_r)):
                    wait_alone(dve, h_mm, i + k + 1, waits_passed)
                    dve.tensor_tensor(h_whole[:, bass.ts(i + k - SPLIT, CHUNKS * F)], ps[0:ROWS, :], bi_all,
                                      ALU.add).then_inc(h_done, 1)

            def ln_stats(src, key, n):
                for c in range(CHUNKS):
                    last = dve.bn_stats(stats[key][:, c, :], src[:, c, :])
                return last

            def ln_start(src, key, prefix, k):
                ln_stats(src, key, k).then_inc(S[prefix + "_stats"], 1)
                wait_alone(dve, S[prefix + "_stats"], done(k + 1), waits_passed)
                for c in range(CHUNKS):
                    last = dve.bn_aggr(mv[key][:, c, :], stats[key][:, c, :])
                last.then_inc(S[prefix + "_aggr"], 1)
                dve.wait_ge(S[prefix + "_aggr"], done(k + 1))
                dve.tensor_scalar(var[key][:, :], mv[key][:, :, 1], LN_EPS, None, ALU.add).then_inc(
                    S[prefix + "_var"], 1)

            def ln_apply(dst, src, key, prefix, k, signal):
                dve.wait_ge(S[prefix + "_rstd"], done(k + 1))
                for c in range(CHUNKS):
                    last = dve.tensor_scalar(dst[:, c, :], src[:, c, :], mv[key][:, c, 0:1], rstd[key][:, c:c + 1],
                                             ALU.subtract, ALU.mult)
                last.then_inc(S[signal], 1)

            def degrees(e):
                dve.wait_ge(S["deg_mm"], done(e + 1))
                dve.tensor_scalar(deg0[:, :], ps_d[0:ROWS, 0:CHUNKS], 1.0, 0.0, ALU.add, ALU.is_equal).then_inc(
                    S["deg_zero"], 1)
                dve.wait_ge(S["deg_zero"], done(e + 1))
                dve.scalar_tensor_tensor(out=deg1[:, :], in0=ps_d[0:ROWS, 0:CHUNKS], scalar=1.0, in1=deg0[:, :],
                                         op0=ALU.add, op1=ALU.add).then_inc(S["deg_safe"], 1)

            def scales(e):
                dve.wait_ge(S["deg_pow"], done(e + 1))
                dve.tensor_tensor(dcur[:, :], dpow[:, :], deg0[:, :], ALU.subtract).then_inc(S["d_cur"], 1)
                wait_alone(dve, S["d_cur"], done(e + 1), waits_passed)
                dve.tensor_copy(d_sb[:, bass.ts(e, CHUNKS)], dcur[:, :]).then_inc(S["d_made"], 1)

            def first_residual(e):
                dve.wait_ge(S["r_turned"], done(e + 1))
                dve.wait_ge(S["xr_in"], loaded(e + 1))
                dve.wait_ge(S["x1_stored"], stored(e))
                dve.tensor_tensor(x1[:, :, :].rearrange("p c f -> p (c f)"), ps_r[0:ROWS, :],
                                  x_in[:, :, :].rearrange("p c f -> p (c f)"), ALU.add).then_inc(S["x1_made"], 1)
                dve.wait_ge(S["x1_made"], done(e + 1))
                ln_start(x1, "2", "l2", e)

            def second_norm(e):
                ln_apply(normed, x1, "2", "l2", e, "h2_norm")

            def second_features(e, split):
                dve.wait_ge(S["sup_mm"], done(e + 1))
                dve.tensor_tensor(normed[:, :, :].rearrange("p c f -> p (c f)"), ps_s[0:ROWS, :], bo_all[:, :],
                                  ALU.add).then_inc(S["sup_bias"], 1)
                dve.wait_ge(S["sup_bias"], done(e + 1))
                for c in range(CHUNKS):
                    last = dve.tensor_scalar(normed[:, c, :], normed[:, c, :], dcur[:, c:c + 1], None, ALU.mult)
                last.then_inc(S["s_scaled"], 1)
                s_e = normed[:, :, :].rearrange("p c f -> p (c f)")
                wait_alone(dve, S["s_scaled"], done(e + 1), waits_passed)
                if split:
                    at = bass.ts(e, CHUNKS * F)
                    dve.tensor_copy(s_high[:, at], s_e).then_inc(S["s_high"], 1)
                    wait_alone(dve, S["s_high"], done(e + 1), waits_passed)
                    dve.tensor_tensor(s_low[:, at], s_e, s_high[:, at].bitcast(F32), ALU.subtract).then_inc(
                        S["s_made"], 1)
                else:
                    dve.tensor_copy(s_whole[:, bass.ts(e - SPLIT, CHUNKS * F)], s_e).then_inc(S["s_made"], 1)
                for c in range(CHUNKS):
                    last = dve.scalar_tensor_tensor(out=x1[:, c, :], in0=normed[:, c, :], scalar=dcur[:, c:c + 1],
                                                    in1=x1[:, c, :], op0=ALU.mult, op1=ALU.add)
                last.then_inc(S["x1s_made"], 1)

            def take_low(m, ring, p, half):
                if not isinstance(m, int) or m >= RING:
                    dve.wait_ge(halves_used, m - RING + 1)
                dve.wait_ge(highs_made, m + 1)
                dve.tensor_tensor(adj_low[ring % RING][:, :], adj_sb[p % SLOTS][0:ROWS, half * HALF:(half + 1) * HALF],
                                  adj_high[ring % RING][:, :].bitcast(F32), ALU.subtract).then_inc(lows_made, 1)

            def pass1(b, section, first):
                n = 0
                for p, g in enumerate(column_blocks(section)):
                    if p == 2:
                        dve.wait_ge(S["xu_in"], loaded(b + 1))
                        ln_start(x_in, "u", "u", b)
                    if p == 3:
                        dve.wait_ge(S["u_turned"], done(b))
                        ln_apply(normed, x_in, "u", "u", b, "u_norm")
                    if not first:
                        if p == 5:
                            degrees(b - 1)
                        if p == 8:
                            first_residual(b - 1)
                        if p == 9:
                            scales(b - 1)
                        if p == 10:
                            dve.wait_ge(S["u_turned"], done(b + 1))
                            second_norm(b - 1)
                        if p == 17:
                            second_features(b - 1, before_is_split(b, section))
                    if is_split(g):
                        for half in range(2):
                            take_low(2 * SPLIT * b + n, n, p, half)
                            n += 1
                    dve.wait_ge(adj_in[p % SLOTS], 16 * (PER_SLOT * b + p // SLOTS + 1))
                    if p == 1:
                        if not first:
                            dve.wait_ge(S["fold_made"], done(b))
                        dve.tensor_tensor(acc[:, :], adj_sb[0][0:ROWS, :], adj_sb[1][0:ROWS, :], ALU.add).then_inc(
                            row_sums, 2)
                    if p > 1:
                        dve.wait_ge(row_sums, BLOCKS * b + p)
                        dve.tensor_tensor(acc[:, :], acc[:, :], adj_sb[p % SLOTS][0:ROWS, :], ALU.add).then_inc(
                            row_sums, 1)
                dve.wait_ge(row_sums, BLOCKS * (b + 1))
                dve.tensor_tensor(acc[:, 0:HALF], acc[:, 0:HALF], acc[:, HALF:], ALU.add).then_inc(S["fold_half"], 1)
                dve.wait_ge(S["fold_half"], done(b + 1))
                dve.wait_ge(S["deg_mm"], done(b))
                dve.tensor_tensor(fold[0:ROWS, :], acc[:, 0:BLOCK], acc[:, BLOCK:HALF], ALU.add).then_inc(
                    S["fold_made"], 1)

            def take_sum(t, v, half):
                dve.wait_ge(halves_used, halves_before(t, v))
                dve.wait_ge(natives_used, natives_before(t, v))
                dve.wait_ge(S["part_in"], loaded(t))
                dve.wait_ge(S["zt_turned"], done(t - 1))
                dve.tensor_tensor(r_t[:, :], z_banks[half][:, 0:BLOCK], part[:, :], ALU.add).then_inc(
                    S["zt_made"], 1)

            def finish(t):
                dve.wait_ge(S["out_stored"], stored(t))
                wait_alone(dve, S["zt_turned"], done(t + 1), waits_passed)
                dve.tensor_copy(dcur[:, :], d_sb[:, bass.ts(BLOCKS - 1 - t, CHUNKS)]).then_inc(S["d_cur"], 1)
                dve.wait_ge(S["d_cur"], done(BLOCKS + t + 1))
                dve.wait_ge(S["x1_in"], loaded(t + 1))
                for c in range(CHUNKS):
                    last = dve.scalar_tensor_tensor(out=normed[:, c, :], in0=ps_r[0:ROWS, c * F:(c + 1) * F],
                                                    scalar=dcur[:, c:c + 1], in1=x1[:, c, :], op0=ALU.mult,
                                                    op1=ALU.add)
                last.then_inc(S["out_made"], 1)

            def pass2(t, v, first, half):
                if first:
                    degrees(BLOCKS - 1)
                    first_residual(BLOCKS - 1)
                    scales(BLOCKS - 1)
                    second_norm(BLOCKS - 1)
                    second_features(BLOCKS - 1, False)
                    for g in range(HELD, BLOCKS):
                        dve.wait_ge(held_high, g - HELD + 1)
                        dve.tensor_tensor(whole_block(h_low, g - HELD), whole_block(s_whole, g - SPLIT),
                                          whole_block(h_high, g - HELD).bitcast(F32), ALU.subtract).then_inc(held_low, 1)
                n = 0
                for p, g in enumerate(second_blocks(v)):
                    if p == 2 and not first:
                        take_sum(t, v, 1 - half)
                    if p == min(7, SECTION * (v + 1) - 1) and not first:
                        finish(t - 1)
                    if second_split(v, g):
                        for h in range(2):
                            take_low(halves_before(t, v) + n, n, p, h)
                            n += 1

            first_pass(dve, pass1)
            second_pass(dve, pass2)
            take_sum(BLOCKS, SECTIONS - 1, (BLOCKS - 1) % 2)
            finish(BLOCKS - 1)

        @block.tensor
        def _(pe):
            for name in ("u_turned", "u_added", "z1_summed", "r_turned", "h2_turned", "sup_mm", "deg_mm",
                         "zt_turned"):
                pe.sem_inc(S[name], 1)
            pe.wait_ge(consts_in, 96)
            pe.wait_ge(consts_set, 4)
            for ps, row in ((ps_u, b_item_row), (ps_h, b_out_row)):
                pe.matmul(ps[0:ROWS, :], ones_row[:, 0:ROWS], row, start=True, stop=True).then_inc(bias_mm, 1)
            def item_block(i, k, ps):
                for c in range(CHUNKS):
                    last = pe.matmul(ps[0:ROWS, c * F:(c + 1) * F], item_sb[k][:, c * ROWS:(c + 1) * ROWS], w_item,
                                     start=True, stop=True)
                last.then_inc(h_mm, 1)

            for k, ps in enumerate((ps_s, ps_r)):
                pe.wait_ge(item_in[k], 16)
                item_block(k, k, ps)
            with pe.Fori(2, BLOCKS - 1, 2) as i:
                for k, ps in enumerate((ps_s, ps_r)):
                    pe.wait_ge(h_done, i + k - 1)
                    pe.wait_ge(item_in[k], 8 * i + 16)
                    item_block(i + k, k, ps)
            pe.wait_ge(h_done, BLOCKS)

            def tile(features, i, c):
                at = (i * CHUNKS + c) * F
                return features[:, at:at + F]

            def native_products(z, features, i, p, starts, ends):
                for c in range(CHUNKS):
                    last = pe.matmul(z[:, 0:BLOCK], tile(features, i, c),
                                     adj_sb[p % SLOTS][0:ROWS, c * BLOCK:(c + 1) * BLOCK],
                                     start=starts and c == 0, stop=ends and c == CHUNKS - 1)
                return last

            def split_products(z, high, low, i, ring, half, starts, ends):
                a_high, a_low = adj_high[ring % RING], adj_low[ring % RING]
                for j in range(CHUNKS // 2):
                    c = half * CHUNKS // 2 + j
                    at = slice(j * BLOCK, (j + 1) * BLOCK)
                    pe.matmul(z[:, 0:BLOCK], tile(high, i, c), a_high[:, at], start=starts and c == 0, stop=False)
                    pe.matmul(z[:, 0:BLOCK], tile(low, i, c), a_high[:, at], start=False, stop=False)
                    last = pe.matmul(z[:, 0:BLOCK], tile(high, i, c), a_low[:, at], start=False,
                                     stop=ends and c == CHUNKS - 1)
                return last

            def turn_rows(ps, src, signal):
                for c in range(CHUNKS):
                    last = pe.transpose(ps[:, c * ROWS:(c + 1) * ROWS], src[:, c, :], ident[0:ROWS, 0:ROWS])
                last.then_inc(S[signal], 1)

            def turn_back(ps, src, signal):
                for c in range(CHUNKS):
                    last = pe.transpose(ps[0:ROWS, c * F:(c + 1) * F], src[:, c * ROWS:(c + 1) * ROWS], ident[:, :])
                last.then_inc(S[signal], 1)

            def degree_sums(e):
                pe.wait_ge(S["fold_made"], done(e + 1))
                pe.wait_ge(S["deg_safe"], done(e))
                for c in range(CHUNKS):
                    last = pe.matmul(ps_d[0:ROWS, c:c + 1], fold[0:ROWS, c * ROWS:(c + 1) * ROWS], ones_col[0:ROWS, :],
                                     start=True, stop=True)
                last.then_inc(S["deg_mm"], 1)

            def turn_r(e):
                pe.wait_ge(S["r_relu"], done(e + 1))
                pe.wait_ge(S["x1_made"], done(e))
                turn_back(ps_r, r_t, "r_turned")

            def turn_h2(e):
                pe.wait_ge(S["h2_norm"], done(e + 1))
                pe.wait_ge(S["h2_relu"], done(e))
                turn_rows(ps_h, normed, "h2_turned")

            def support(e):
                pe.wait_ge(S["h2_relu"], done(e + 1))
                pe.wait_ge(S["s_made"], done(e))
                for c in range(CHUNKS):
                    last = pe.matmul(ps_s[0:ROWS, c * F:(c + 1) * F], turned[:, c * ROWS:(c + 1) * ROWS], wo[:, :],
                                     start=True, stop=True)
                last.then_inc(S["sup_mm"], 1)

            def pass1(b, section, first):
                order = column_blocks(section)
                known = SECTION * section
                both = [p for p, g in enumerate(order) if g < known]
                n = 0
                if not first:
                    pe.wait_ge(S["r_relu"], done(b))
                for p, g in enumerate(order):
                    ends = p == BLOCKS - 1
                    pe.wait_ge(adj_in[p % SLOTS], 16 * (PER_SLOT * b + p // SLOTS + 1))
                    if p in both[:1]:
                        pe.wait_ge(S["part_made"], done(b - SECTION))
                        pe.wait_ge(S["s_made"], done(known - 1))
                    if ends and section:
                        pe.wait_ge(S["s_made"], done(known))
                    if is_split(g):
                        for half in range(2):
                            pe.wait_ge(lows_made, 2 * SPLIT * b + n + 1)
                            last = split_products(z1, h_high, h_low, g, n, half, p == 0, ends)
                            if ends and half and section:
                                last.then_inc(S["z1_summed"], 1)
                            if g < known:
                                last = split_products(z2, s_high, s_low, g, n, half, p == both[0], ends)
                            last.then_inc(halves_used, 1)
                            n += 1
                    else:
                        last = native_products(z1, h_whole, g - SPLIT, p, p == 0, ends)
                        if ends and section:
                            last.then_inc(S["z1_summed"], 1)
                        if g < known:
                            last = native_products(z2, s_whole, g - SPLIT, p, p == both[0], ends)
                        last.then_inc(natives_used, 1)
                    if p == 4:
                        pe.wait_ge(S["u_norm"], done(b + 1))
                        pe.wait_ge(S["u_relu"], done(b))
                        turn_rows(ps_u, normed, "u_turned")
                    if p == 8:
                        pe.wait_ge(S["u_relu"], done(b + 1))
                        pe.matmul(z1[:, 0:BLOCK], wu[:, :], turned[:, :], start=False, stop=False).then_inc(
                            S["u_added"], 1)
                    if not first:
                        if p == 1:
                            degree_sums(b - 1)
                        if p == 5:
                            turn_r(b - 1)
                        if p == 10:
                            turn_h2(b - 1)
                        if p == 14:
                            support(b - 1)

            def pass2(t, v, first, half):
                order = second_blocks(v)
                z = z_banks[half]
                if first:
                    degree_sums(BLOCKS - 1)
                    pe.wait_ge(S["r_relu"], done(BLOCKS))
                    pe.wait_ge(S["part_made"], done(BLOCKS - SECTION))
                elif not (v == 0 and t < 2):
                    pe.wait_ge(S["zt_made"], done(t - 1))
                if v == 1:
                    pe.wait_ge(held_low, SPLIT)
                n = 0
                for p, g in enumerate(order):
                    starts, ends = p == 0, p == len(order) - 1
                    pe.wait_ge(adj_in[p % SLOTS], 16 * (second_loads(t, v, p) + 1))
                    if first and ends:
                        support(BLOCKS - 1)
                        pe.wait_ge(S["s_made"], done(BLOCKS))
                    if second_split(v, g):
                        high, low, i = (s_high, s_low, g) if is_split(g) else (h_high, h_low, g - HELD)
                        for h in range(2):
                            pe.wait_ge(lows_made, halves_before(t, v) + n + 1)
                            split_products(z, high, low, i, n, h, starts, ends).then_inc(halves_used, 1)
                            n += 1
                    else:
                        native_products(z, s_whole, g - SPLIT, p, starts, ends).then_inc(natives_used, 1)
                    if first and p == 0:
                        turn_r(BLOCKS - 1)
                    if first and p == 1:
                        turn_h2(BLOCKS - 1)
                    if not first and p == 3:
                        turn_sum(t - 1)

            def turn_sum(t):
                pe.wait_ge(S["zt_made"], done(t + 1))
                pe.wait_ge(S["out_made"], done(t))
                turn_back(ps_r, r_t, "zt_turned")

            first_pass(pe, pass1)
            second_pass(pe, pass2)
            turn_sum(BLOCKS - 1)


def build(nc, shapes):
    def dram(name, shape, kind="ExternalInput"):
        return nc.dram_tensor(name, shape, F32, kind=kind).ap()

    args = [dram(n, s) for n, s in shapes]
    out = dram("out_0_dram", (BLOCKS, ROWS, CHUNKS * F), "ExternalOutput")
    gnn_two_layers(nc, *args, out)


def kernel(x, adj, L0_gnn_item_feat, L0_gnn_W_item, L0_gnn_b_item, L0_gnn_W_user, L0_gnn_b_user, L1_gnn_W, L1_gnn_b):
    import numpy as np
    import concourse.bacc as bacc
    from concourse.bass_utils import run_bass_kernel_spmd

    def by_chunks(a):
        return np.ascontiguousarray(a.reshape(BLOCKS, CHUNKS, ROWS, F).transpose(0, 2, 1, 3)).reshape(
            BLOCKS, ROWS, CHUNKS * F)

    adj = np.asarray(adj)
    adj_t = np.zeros((BLOCKS, BLOCKS, 128, CHUNKS, BLOCK), adj.dtype)
    adj_t[:, :, :ROWS] = adj.reshape(BLOCKS, BLOCK, BLOCKS, CHUNKS, ROWS).transpose(0, 2, 4, 3, 1)
    arrays = {
        "in_x": by_chunks(np.asarray(x)),
        "in_adj_t": adj_t.reshape(BLOCKS, BLOCKS, 128, GROUP),
        "in_item_t": np.ascontiguousarray(np.asarray(L0_gnn_item_feat).reshape(BLOCKS, BLOCK, F).transpose(0, 2, 1)),
        "in_w_item_t": np.ascontiguousarray(np.asarray(L0_gnn_W_item).T),
        "in_b_item": np.tile(np.asarray(L0_gnn_b_item), CHUNKS).reshape(1, CHUNKS * F),
        "in_w_user_t": np.ascontiguousarray(np.asarray(L0_gnn_W_user).T),
        "in_b_user": np.asarray(L0_gnn_b_user).reshape(F, 1),
        "in_w_out_t": np.ascontiguousarray(np.asarray(L1_gnn_W).T),
        "in_b_out": np.tile(np.asarray(L1_gnn_b), CHUNKS).reshape(1, CHUNKS * F),
    }
    nc = bacc.Bacc("TRN2", target_bir_lowering=False, num_devices=1)
    build(nc, [(n, a.shape) for n, a in arrays.items()])
    r = run_bass_kernel_spmd(nc, [arrays], core_ids=[0])
    got = r.results[0]["out_0_dram"]
    return got.reshape(BLOCKS, ROWS, CHUNKS, F).transpose(0, 2, 1, 3).reshape(N, F)
```

```python
import concourse.bass as bass
from concourse import mybir
from contextlib import ExitStack

F32 = mybir.dt.float32
F32R = mybir.dt.float32r
ALU = mybir.AluOpType
ACT = mybir.ActivationFunctionType

N = 10000
F = 128
ROWS = 125
CHUNKS = 4
BLOCK = ROWS * CHUNKS
BLOCKS = N // BLOCK
GROUP = CHUNKS * BLOCK
SECTION = 4
SECTIONS = BLOCKS // SECTION
SLOTS = 4
PER_SLOT = BLOCKS // SLOTS
PARTED = 12
WHOLE = BLOCKS - PARTED
HELD = [6, 8, PARTED, PARTED, PARTED]
FRESH = [(), (), (), (12, 13, 14, 16), (12, 13, 14, 16)]
SPLITS = [held + len(fresh) for held, fresh in zip(HELD, FRESH)]
LATER = range(min(HELD), PARTED)
SCRATCH = 1024
HALF = GROUP // 2
RING = 4
LN_EPS = 1e-5


def done(n):
    return n + 1


def stored(n):
    return 16 * (n + 1)


def loaded(n):
    return 16 * n


def wait_alone(eng, semaphore, value, passed):
    eng.wait_ge(semaphore, value)
    eng.sem_inc(passed, 1)


def is_split(g, section):
    return g < HELD[section] or g in FRESH[section]


def fresh_before(b, section):
    per_block = [sum(2 if g < SECTION * q else 1 for g in fresh) for q, fresh in enumerate(FRESH)]
    return SECTION * sum(per_block[:section]) + per_block[section] * (b - SECTION * section)


def halves_until(b, section):
    return 2 * (SECTION * sum(SPLITS[:section]) + SPLITS[section] * (b - SECTION * section))


def natives_until(b, section):
    return (SECTION * (BLOCKS * section - sum(SPLITS[:section]))
            + (BLOCKS - SPLITS[section]) * (b - SECTION * section))


def tensor_lead(g, section):
    layers = 2 if g < SECTION * section else 1
    return layers * (3 if is_split(g, section) else 4) * CHUNKS - (20 if is_split(g, section) else 12)


def column_blocks(section):
    known = SECTION * section
    last = [known - 1] if section else []
    natives = [g for g in range(known, BLOCKS) if not is_split(g, section)]
    out = natives[:3]
    left = [g for g in range(BLOCKS) if g not in out + last]
    n, lead = len(left), 0
    share = sum(tensor_lead(g, section) for g in left) / n
    for i in range(n):
        turn = (i + 2) * len(FRESH[section]) // n > sum(g in FRESH[section] for g in out)
        choice = [g for g in left if (g in FRESH[section]) == turn]
        best = min(choice or left, key=lambda g: (abs(lead + tensor_lead(g, section) - share * (i + 1)), g))
        left.remove(best)
        lead += tensor_lead(best, section)
        out.append(best)
    return out + last


def second_split(v, g):
    return v > 0


def second_blocks(v):
    return list(range(BLOCKS - SECTION * (v + 1), BLOCKS))


def splits_in(v):
    return sum(second_split(v, g) for g in second_blocks(v))


def halves_before(t, v):
    return (halves_until(BLOCKS, SECTIONS - 1)
            + 2 * (SECTION * sum(splits_in(u) for u in range(v)) + splits_in(v) * (t - SECTION * v)))


def natives_before(t, v):
    natives = [SECTION * (u + 1) - splits_in(u) for u in range(v + 1)]
    return natives_until(BLOCKS, SECTIONS - 1) + SECTION * sum(natives[:v]) + natives[v] * (t - SECTION * v)


def loads_before(section_index):
    return PER_SLOT * BLOCKS + SECTION * section_index * (section_index + 1) // 2


def gnn_two_layers(nc, x, adj_t, item_t, w_item_t, b_item4, w_user_t, b_user, w_out_t, b_out4, out):
    ctx = ExitStack()
    with ctx:
        def sb(name, shape, dt=F32):
            return ctx.enter_context(nc.sbuf_tensor(name, shape, dt))

        def bank(name):
            return ctx.enter_context(nc.psum_tensor(name, [128, 512], F32))

        def sem(name):
            return ctx.enter_context(nc.semaphore(name))

        x1_dram = nc.dram_tensor("x1_dram", (BLOCKS, ROWS, CHUNKS * F), F32, kind="Internal").ap()
        part_dram = nc.dram_tensor("part_dram", (BLOCKS, F, BLOCK), F32, kind="Internal").ap()

        h_high = sb("h_high", [ROWS, PARTED * CHUNKS * F], F32R)
        h_low = sb("h_low", [ROWS, PARTED * CHUNKS * F], F32R)
        h_whole = sb("h_whole", [ROWS, WHOLE * CHUNKS * F])
        s_high = sb("s_high", [ROWS, PARTED * CHUNKS * F], F32R)
        s_low = sb("s_low", [ROWS, PARTED * CHUNKS * F], F32R)
        s_whole = sb("s_whole", [ROWS, WHOLE * CHUNKS * F])
        adj_high = [sb(f"adj_high{i}", [ROWS, HALF], F32R) for i in range(RING)]
        adj_low = [sb(f"adj_low{i}", [ROWS, HALF], F32R) for i in range(RING)]
        d_sb = sb("d_sb", [ROWS, BLOCKS * CHUNKS])
        adj_sb = [sb(f"adj{i}", [128, GROUP]) for i in range(SLOTS)]
        acc = sb("acc", [128, GROUP])
        fresh_high = [sb(f"fresh_high{i}", [ROWS, CHUNKS * F], F32R) for i in range(2)]
        fresh_low = [sb(f"fresh_low{i}", [ROWS, CHUNKS * F], F32R) for i in range(2)]

        ident = sb("ident", [128, 128])
        ones_col = sb("ones_col", [128, 1])
        minus_half = sb("minus_half", [ROWS, CHUNKS])
        wu = sb("wu", [F, F])
        wo = sb("wo", [F, F])
        bu = sb("bu", [F, 1])
        bo_all = sb("bo_all", [ROWS, CHUNKS * F])

        x_in = sb("x_in", [ROWS, CHUNKS, F])
        normed = sb("normed", [ROWS, CHUNKS, F])
        x1 = sb("x1", [ROWS, CHUNKS, F])
        turned = sb("turned", [F, BLOCK])
        r_t = sb("r_t", [F, BLOCK])
        part = sb("part", [F, BLOCK])
        fold = turned
        w_item = fold[:, 0:F]
        ones_row = fold[0:1, F:2 * F]
        items = [adj_sb[2], adj_sb[3], acc, adj_sb[2], adj_sb[3]]
        bi_all = x1[:, :, :].rearrange("p c f -> p (c f)")
        h_tmp = [normed[:, :, :].rearrange("p c f -> p (c f)"), x_in[:, :, :].rearrange("p c f -> p (c f)")]
        b_item_row, b_out_row = h_tmp[0][0:1, :], h_tmp[1][0:1, :]
        stats = {k: sb(f"stats_{k}", [ROWS, CHUNKS, 6]) for k in "u2"}
        shift = {k: sb(f"shift_{k}", [ROWS, CHUNKS]) for k in "u2"}
        mv = {k: sb(f"mv_{k}", [ROWS, CHUNKS, 2]) for k in "u2"}
        var = {k: sb(f"var_{k}", [ROWS, CHUNKS]) for k in "u2"}
        rstd = {k: sb(f"rstd_{k}", [ROWS, CHUNKS]) for k in "u2"}
        deg0 = sb("deg0", [ROWS, CHUNKS])
        deg1 = sb("deg1", [ROWS, CHUNKS])
        dpow = sb("dpow", [ROWS, CHUNKS])
        dcur = sb("dcur", [ROWS, CHUNKS])

        z1, z2, ps_u, ps_r, ps_h, ps_s, ps_d = (bank(n) for n in ("z1", "z2", "ps_u", "ps_r", "ps_h", "ps_s", "ps_d"))
        z_banks = [z1, z2]
        h_banks = [ps_s, ps_r, z1, z2]

        consts_in = sem("consts_in")
        consts_set = sem("consts_set")
        w_item_in = sem("w_item_in")
        bias_rows_in = sem("bias_rows_in")
        ident_zero = sem("ident_zero")
        item_in = [sem(f"item_in{i}") for i in range(len(items))]
        bias_mm = sem("bias_mm")
        bias_done = sem("bias_done")
        h_mm = sem("h_mm")
        adj_in = [sem(f"adj_in{i}") for i in range(SLOTS)]
        highs_made = sem("highs_made")
        lows_made = sem("lows_made")
        fresh_highs = sem("fresh_highs")
        fresh_lows = sem("fresh_lows")
        halves_used = sem("halves_used")
        natives_used = sem("natives_used")
        row_sums = sem("row_sums")
        waits_passed = sem("waits_passed")

        STAGES = ("u_stats", "u_aggr", "u_var", "u_rstd", "u_shift", "u_norm", "u_turned", "u_relu", "u_added",
                  "z1_summed", "r_relu", "r_turned", "x1_made", "l2_stats", "l2_aggr", "l2_var", "l2_rstd", "l2_shift",
                  "h2_norm", "h2_turned", "h2_relu", "sup_mm", "sup_bias", "s_scaled", "s_high", "s_made",
                  "fold_half", "fold_made", "deg_mm", "deg_zero", "deg_safe", "deg_pow", "d_cur", "d_made",
                  "part_made", "zt_made", "zt_turned", "out_made")
        STAGES_DMA = ("xu_in", "xr_in", "x1_stored", "part_stored", "part_in", "x1_in", "out_stored")
        S = {n: sem(n) for n in STAGES + STAGES_DMA}
        part_zero = sem("part_zero")
        h_sum = sem("h_sum")
        h_high_made = sem("h_high_made")
        h_low_made = sem("h_low_made")
        held_high = sem("held_high")
        held_low = sem("held_low")

        block = ctx.enter_context(nc.Block())

        def first_pass(eng, body):
            cuts = sorted({0, 1, PARTED, PARTED + 1} | {SECTION * q for q in range(1, SECTIONS + 1)})
            for lo, hi in zip(cuts[:-1], cuts[1:]):
                if hi - lo == 1:
                    body(lo, lo // SECTION, lo == 0)
                else:
                    with eng.Fori(lo, hi) as b:
                        body(b, lo // SECTION, False)

        def before_is_parted(b, section):
            return b <= PARTED if isinstance(b, int) else section < PARTED // SECTION

        def fresh_features(g, section):
            if g not in FRESH[section]:
                return []
            return [(0, h_whole, g - PARTED)] + ([(1, s_whole, g - PARTED)] if g < SECTION * section else [])

        def later_whole(g):
            return WHOLE - len(LATER) + g - LATER[0]

        def second_pass(eng, body):
            for t in range(SECTION):
                body(t, 0, t == 0, t % 2)
            for v in range(1, SECTIONS):
                with eng.Fori(SECTION * v, SECTION * (v + 1) - 1, 2) as t:
                    body(t, v, False, 0)
                    body(t + 1, v, False, 1)

        def whole_block(features, i):
            return features[:, i * CHUNKS * F:(i + 1) * CHUNKS * F]

        def h_of(i):
            return whole_block(s_whole, later_whole(i)) if i in LATER else h_tmp[i % 2]

        def second_loads(t, v, p):
            return loads_before(v) + (v + 1) * (t - SECTION * v) + p // SLOTS

        @block.sync
        def _(sp):
            sp.dma_start(w_item, w_item_t).then_inc(w_item_in, 16)
            for i in range(3):
                sp.dma_start(items[i][:, :], item_t[i]).then_inc(item_in[i], 16)
            for dst, src in ((wu[:, :], w_user_t), (wo[:, :], w_out_t), (bu[:, :], b_user)):
                sp.dma_start(dst, src).then_inc(consts_in, 16)

            def natives_up_to(section, p):
                return sum(not is_split(g, section) for g in column_blocks(section)[:p + 1])

            def pass1(b, section, first):
                for p, g in enumerate(column_blocks(section)):
                    if not (first and p < SLOTS):
                        wait_alone(sp, row_sums, BLOCKS * b + p - SLOTS + 1, waits_passed)
                        if p >= SLOTS:
                            natives = natives_until(b, section) + natives_up_to(section, p - SLOTS)
                        else:
                            natives = natives_until(b, section) - min(
                                BLOCKS - SPLITS[q] - natives_up_to(q, BLOCKS - SLOTS + p)
                                for q in (max(section - 1, 0), section))
                        if not first or natives > 0:
                            wait_alone(sp, natives_used, natives, waits_passed)
                    if first and p == 2:
                        for q in (2, 3):
                            sp.wait_ge(h_mm, CHUNKS * (q - 1))
                            sp.dma_start(items[q + 1][:, :], item_t[q + 1]).then_inc(item_in[q + 1], 16)
                    if first and p in (2, 3):
                        sp.wait_ge(h_mm, CHUNKS * (p + 2))
                    sp.dma_start(adj_sb[p % SLOTS][:, :], adj_t[b, g]).then_inc(adj_in[p % SLOTS], 16)

            def pass2(t, v, first, half):
                order = second_blocks(v)
                for p, g in enumerate(order):
                    if first:
                        sp.wait_ge(row_sums, BLOCKS * BLOCKS - SLOTS + 1 + p)
                        sp.wait_ge(natives_used, natives_until(BLOCKS - 1, SECTIONS - 1)
                                   + natives_up_to(SECTIONS - 1, BLOCKS - SLOTS + p))
                    elif v == 0:
                        sp.wait_ge(natives_used, natives_before(t - 1, v) + p + 1)
                    else:
                        if p < SLOTS:
                            natives = natives_before(t, v) - (SLOTS - 1 - p)
                            halves = halves_before(t, v) - 2 * (SLOTS - 1 - p)
                        else:
                            natives = natives_before(t, v) + sum(not second_split(v, q) for q in order[:p - SLOTS + 1])
                            halves = halves_before(t, v) + 2 * sum(second_split(v, q) for q in order[:p - SLOTS + 1])
                        wait_alone(sp, natives_used, natives, waits_passed)
                        wait_alone(sp, lows_made, halves, waits_passed)
                    sp.dma_start(adj_sb[p % SLOTS][:, :], adj_t[BLOCKS - 1 - t, g]).then_inc(adj_in[p % SLOTS], 16)

            first_pass(sp, pass1)
            second_pass(sp, pass2)

        @block.gpsimd
        def _(pool):
            for name in ("u_rstd", "l2_rstd", "deg_pow"):
                pool.sem_inc(S[name], 1)
            pool.memset(ident[:, :], 0.0).then_inc(ident_zero, 1)
            pool.memset(ones_col[:, :], 1.0).then_inc(consts_set, 1)
            pool.memset(ones_row, 1.0).then_inc(consts_set, 1)
            pool.memset(minus_half[:, :], -0.5).then_inc(consts_set, 1)
            pool.wait_ge(ident_zero, 1)
            pool.affine_select(out=ident[:, :], in_=ident[:, :], compare_op=ALU.not_equal, fill=1.0, base=0,
                               pattern=[[-1, 128]], channel_multiplier=1).then_inc(consts_set, 1)
            pool.wait_ge(consts_set, 4)

            def power(dst, src, wait_on, signal, k):
                pool.wait_ge(S[wait_on], done(k + 1))
                pool.tensor_tensor(dst[:, :], src[:, :], minus_half[:, :], ALU.pow).then_inc(S[signal], 1)

            def load_x(dst, src, signal):
                pool.dma_start(dst[:, :, :].rearrange("p c f -> p (c f)"), src).then_inc(S[signal], 16)

            def end_of_block(e):
                load_x(x_in, x[e], "xr_in")
                power(dpow, deg1, "deg_safe", "deg_pow", e)
                power(rstd["2"], var["2"], "l2_var", "l2_rstd", e)

            def pass1(b, section, first):
                if first:
                    pool.wait_ge(h_high_made, PARTED)
                    pool.wait_ge(h_low_made, PARTED)
                else:
                    wait_alone(pool, S["u_norm"], done(b), waits_passed)
                    wait_alone(pool, S["x1_made"], done(b - 1), waits_passed)
                load_x(x_in, x[b], "xu_in")
                power(rstd["u"], var["u"], "u_var", "u_rstd", b)
                if not first:
                    wait_alone(pool, S["u_norm"], done(b + 1), waits_passed)
                    end_of_block(b - 1)

            def pass2(t, v, first, half):
                if first:
                    wait_alone(pool, S["x1_made"], done(BLOCKS - 1), waits_passed)
                    end_of_block(BLOCKS - 1)
                    pool.wait_ge(S["x1_stored"], stored(BLOCKS))
                    pool.wait_ge(S["part_stored"], loaded(BLOCKS))
                wait_alone(pool, S["zt_made"], done(t), waits_passed)
                pool.dma_start(part[:, :], part_dram[BLOCKS - 1 - t]).then_inc(S["part_in"], 16)
                wait_alone(pool, S["out_made"], done(t), waits_passed)
                load_x(x1, x1_dram[BLOCKS - 1 - t], "x1_in")

            first_pass(pool, pass1)
            second_pass(pool, pass2)

        @block.scalar
        def _(act):
            for dst, src in ((b_item_row, b_item4), (b_out_row, b_out4)):
                act.dma_start(dst, src).then_inc(bias_rows_in, 16)
            for name in ("u_relu", "r_relu", "h2_relu", "part_made", "u_norm", "h2_norm", "s_scaled", "s_high"):
                act.sem_inc(S[name], 1)
            for name in ("x1_stored", "out_stored"):
                act.sem_inc(S[name], 16)
            act.wait_ge(part_zero, 1)
            for b in range(SECTION):
                act.dma_start(part_dram[b], part[:, :]).then_inc(S["part_stored"], 16)
            act.wait_ge(consts_in, 48)
            for i in range(PARTED):
                act.wait_ge(h_sum, i + 1)
                act.activation(whole_block(h_high, i), h_of(i), ACT.Copy).then_inc(h_high_made, 1)

            def apply_norm(src, key, prefix, k, signal):
                act.wait_ge(S[prefix + "_shift"], done(k + 1))
                for c in range(CHUNKS):
                    last = act.activation(normed[:, c, :], src[:, c, :], ACT.Identity, bias=shift[key][:, c:c + 1],
                                          scale=rstd[key][:, c:c + 1])
                last.then_inc(S[signal], 1)

            def scale_s(e, split):
                act.wait_ge(S["sup_bias"], done(e + 1))
                for c in range(CHUNKS):
                    last = act.activation(normed[:, c, :], normed[:, c, :], ACT.Copy, scale=dcur[:, c:c + 1])
                last.then_inc(S["s_scaled"], 1)
                act.wait_ge(S["s_scaled"], done(e + 1))
                to = s_high[:, bass.ts(e, CHUNKS * F)] if split else s_whole[:, bass.ts(e - PARTED, CHUNKS * F)]
                act.activation(to, normed[:, :, :].rearrange("p c f -> p (c f)"), ACT.Copy).then_inc(S["s_high"], 1)

            def round_half(m, ring, p, half):
                if not isinstance(m, int) or m >= RING:
                    act.wait_ge(halves_used, m - RING + 1)
                act.activation(adj_high[ring % RING][:, :], adj_sb[p % SLOTS][0:ROWS, half * HALF:(half + 1) * HALF],
                               ACT.Copy).then_inc(highs_made, 1)

            def store_x1(e):
                act.wait_ge(S["s_made"], done(e + 1))
                act.dma_start(x1_dram[e], x1[:, :, :].rearrange("p c f -> p (c f)")).then_inc(S["x1_stored"], 16)

            def relu_h2(e):
                act.wait_ge(S["h2_turned"], done(e + 1))
                act.activation(turned[:, :], ps_h[:, 0:BLOCK], ACT.Relu).then_inc(S["h2_relu"], 1)

            def pass1(b, section, first):
                n = 0
                fresh_used = 0
                for p, g in enumerate(column_blocks(section)):
                    if p == 4:
                        if not first:
                            act.wait_ge(S["s_made"], done(b - 1))
                        apply_norm(x_in, "u", "u", b, "u_norm")
                    if p == 8:
                        act.wait_ge(S["u_turned"], done(b + 1))
                        if not first:
                            act.wait_ge(S["sup_mm"], done(b - 1))
                        act.activation(turned[:, :], ps_u[:, 0:BLOCK], ACT.Relu).then_inc(S["u_relu"], 1)
                    if p == 10 and not first:
                        apply_norm(x1, "2", "l2", b - 1, "h2_norm")
                    if p == 13 and not first:
                        act.wait_ge(S["u_added"], done(b + 1))
                        relu_h2(b - 1)
                    if p == 17 and not first:
                        scale_s(b - 1, before_is_parted(b, section))
                    if p == BLOCKS - 1 and not first:
                        store_x1(b - 1)
                    for layer, features, i in fresh_features(g, section):
                        act.wait_ge(halves_used, halves_until(b, section) + fresh_used)
                        act.activation(fresh_high[layer][:, :], whole_block(features, i), ACT.Copy).then_inc(
                            fresh_highs, 1)
                    if is_split(g, section):
                        if g in FRESH[section]:
                            fresh_used = n + 2
                        act.wait_ge(adj_in[p % SLOTS], 16 * (PER_SLOT * b + p // SLOTS + 1))
                        for half in range(2):
                            round_half(halves_until(b, section) + n, n, p, half)
                            n += 1
                if section:
                    act.wait_ge(S["z1_summed"], done(b - SECTION + 1))
                else:
                    act.wait_ge(halves_used, halves_until(b + 1, section))
                    act.wait_ge(natives_used, natives_until(b + 1, section))
                act.wait_ge(S["r_turned"], done(b))
                act.activation(r_t[:, :], z1[:, 0:BLOCK], ACT.Relu, bias=bu[:, 0:1]).then_inc(S["r_relu"], 1)
                if section:
                    act.wait_ge(halves_used, halves_until(b + 1, section))
                    act.wait_ge(natives_used, natives_until(b + 1, section))
                    act.wait_ge(S["part_stored"], loaded(b))
                    act.activation(part[:, :], z2[:, 0:BLOCK], ACT.Copy).then_inc(S["part_made"], 1)
                    act.wait_ge(S["part_made"], done(b - SECTION + 1))
                    act.dma_start(part_dram[b], part[:, :]).then_inc(S["part_stored"], 16)

            def store_out(t):
                act.wait_ge(S["out_made"], done(t + 1))
                act.dma_start(out[BLOCKS - 1 - t], normed[:, :, :].rearrange("p c f -> p (c f)")).then_inc(
                    S["out_stored"], 16)

            def pass2(t, v, first, half):
                if first:
                    apply_norm(x1, "2", "l2", BLOCKS - 1, "h2_norm")
                    relu_h2(BLOCKS - 1)
                    scale_s(BLOCKS - 1, False)
                    store_x1(BLOCKS - 1)
                    act.wait_ge(halves_used, halves_until(BLOCKS, SECTIONS - 1))
                    for g in range(WHOLE):
                        act.activation(whole_block(h_high, g), whole_block(s_whole, g), ACT.Copy).then_inc(held_high, 1)
                n = 0
                for p, g in enumerate(second_blocks(v)):
                    if p == (9 if v > 1 else 7 if v else 3) and not first:
                        store_out(t - 1)
                    if second_split(v, g):
                        act.wait_ge(adj_in[p % SLOTS], 16 * (second_loads(t, v, p) + 1))
                        for h in range(2):
                            round_half(halves_before(t, v) + n, n, p, h)
                            n += 1

            first_pass(act, pass1)
            second_pass(act, pass2)
            store_out(BLOCKS - 1)
            act.wait_ge(S["out_stored"], stored(BLOCKS))

        @block.vector
        def _(dve):
            for name in ("u_stats", "u_aggr", "u_var", "u_shift", "x1_made", "l2_stats", "l2_aggr", "l2_var",
                         "l2_shift", "sup_bias", "s_made", "fold_half",
                         "fold_made", "deg_zero", "deg_safe", "d_cur", "d_made", "zt_made", "out_made"):
                dve.sem_inc(S[name], 1)
            dve.memset(part[:, :], 0.0).then_inc(part_zero, 1)
            dve.wait_ge(bias_mm, 2)
            dve.tensor_copy(bi_all, ps_u[0:ROWS, :]).then_inc(bias_done, 1)
            dve.tensor_copy(bo_all[:, :], ps_h[0:ROWS, :]).then_inc(bias_done, 1)
            dve.wait_ge(bias_done, 2)

            for i in range(BLOCKS):
                to = h_of(i) if i < PARTED else whole_block(h_whole, i - PARTED)
                if 2 <= i < PARTED:
                    dve.wait_ge(h_low_made, i - 1)
                dve.wait_ge(h_mm, i + 1)
                dve.tensor_tensor(to, h_banks[i % 4][0:ROWS, :], bi_all, ALU.add).then_inc(h_sum, 1)
                j = i - 1
                if 0 <= j < PARTED:
                    dve.wait_ge(h_high_made, j + 1)
                    dve.tensor_tensor(whole_block(h_low, j), h_of(j), whole_block(h_high, j).bitcast(F32),
                                      ALU.subtract).then_inc(h_low_made, 1)

            def ln_start(src, key, prefix, k):
                for c in range(CHUNKS):
                    last = dve.bn_stats(stats[key][:, c, :], src[:, c, :])
                last.then_inc(S[prefix + "_stats"], 1)
                wait_alone(dve, S[prefix + "_stats"], done(k + 1), waits_passed)
                for c in range(CHUNKS):
                    last = dve.bn_aggr(mv[key][:, c, :], stats[key][:, c, :])
                last.then_inc(S[prefix + "_aggr"], 1)
                dve.wait_ge(S[prefix + "_aggr"], done(k + 1))
                dve.tensor_scalar(var[key][:, :], mv[key][:, :, 1], LN_EPS, None, ALU.add).then_inc(
                    S[prefix + "_var"], 1)

            def ln_shift(key, prefix, k):
                dve.wait_ge(S[prefix + "_rstd"], done(k + 1))
                dve.scalar_tensor_tensor(out=shift[key][:, :], in0=mv[key][:, :, 0], scalar=-1.0, in1=rstd[key][:, :],
                                         op0=ALU.mult, op1=ALU.mult).then_inc(S[prefix + "_shift"], 1)

            def degrees(e):
                dve.wait_ge(S["deg_mm"], done(e + 1))
                dve.tensor_scalar(deg0[:, :], ps_d[0:ROWS, 0:CHUNKS], 1.0, 0.0, ALU.add, ALU.is_equal).then_inc(
                    S["deg_zero"], 1)
                dve.wait_ge(S["deg_zero"], done(e + 1))
                dve.scalar_tensor_tensor(out=deg1[:, :], in0=ps_d[0:ROWS, 0:CHUNKS], scalar=1.0, in1=deg0[:, :],
                                         op0=ALU.add, op1=ALU.add).then_inc(S["deg_safe"], 1)

            def scales(e):
                dve.wait_ge(S["deg_pow"], done(e + 1))
                dve.tensor_tensor(dcur[:, :], dpow[:, :], deg0[:, :], ALU.subtract).then_inc(S["d_cur"], 1)
                wait_alone(dve, S["d_cur"], done(e + 1), waits_passed)
                dve.tensor_copy(d_sb[:, bass.ts(e, CHUNKS)], dcur[:, :]).then_inc(S["d_made"], 1)

            def first_residual(e):
                dve.wait_ge(S["r_turned"], done(e + 1))
                dve.wait_ge(S["xr_in"], loaded(e + 1))
                dve.wait_ge(S["x1_stored"], stored(e))
                dve.tensor_tensor(x1[:, :, :].rearrange("p c f -> p (c f)"), ps_r[0:ROWS, :],
                                  x_in[:, :, :].rearrange("p c f -> p (c f)"), ALU.add).then_inc(S["x1_made"], 1)
                dve.wait_ge(S["x1_made"], done(e + 1))
                ln_start(x1, "2", "l2", e)

            def support_bias(e):
                dve.wait_ge(S["sup_mm"], done(e + 1))
                dve.tensor_tensor(normed[:, :, :].rearrange("p c f -> p (c f)"), ps_s[0:ROWS, :], bo_all[:, :],
                                  ALU.add).then_inc(S["sup_bias"], 1)

            def second_features(e, split):
                if split:
                    at = bass.ts(e, CHUNKS * F)
                    wait_alone(dve, S["s_high"], done(e + 1), waits_passed)
                    dve.tensor_tensor(s_low[:, at], normed[:, :, :].rearrange("p c f -> p (c f)"),
                                      s_high[:, at].bitcast(F32), ALU.subtract)
                dve.wait_ge(S["s_scaled"], done(e + 1))
                dve.wait_ge(S["s_high"], done(e + 1))
                for c in range(CHUNKS):
                    last = dve.scalar_tensor_tensor(out=x1[:, c, :], in0=normed[:, c, :], scalar=dcur[:, c:c + 1],
                                                    in1=x1[:, c, :], op0=ALU.mult, op1=ALU.add)
                last.then_inc(S["s_made"], 1)

            def take_low(m, ring, p, half):
                if not isinstance(m, int) or m >= RING:
                    dve.wait_ge(halves_used, m - RING + 1)
                dve.wait_ge(highs_made, m + 1)
                dve.tensor_tensor(adj_low[ring % RING][:, :], adj_sb[p % SLOTS][0:ROWS, half * HALF:(half + 1) * HALF],
                                  adj_high[ring % RING][:, :].bitcast(F32), ALU.subtract).then_inc(lows_made, 1)

            def pass1(b, section, first):
                n = 0
                fresh = 0
                for p, g in enumerate(column_blocks(section)):
                    if p == 2:
                        dve.wait_ge(S["xu_in"], loaded(b + 1))
                        ln_start(x_in, "u", "u", b)
                    if p == 3:
                        ln_shift("u", "u", b)
                    if not first:
                        if p == 5:
                            degrees(b - 1)
                        if p == 7:
                            first_residual(b - 1)
                        if p == 8:
                            scales(b - 1)
                        if p == 9:
                            ln_shift("2", "l2", b - 1)
                        if p == 16:
                            support_bias(b - 1)
                        if p == 18:
                            second_features(b - 1, before_is_parted(b, section))
                    for layer, features, i in fresh_features(g, section):
                        fresh += 1
                        wait_alone(dve, fresh_highs, fresh_before(b, section) + fresh, waits_passed)
                        dve.tensor_tensor(fresh_low[layer][:, :], whole_block(features, i),
                                          fresh_high[layer][:, :].bitcast(F32), ALU.subtract).then_inc(fresh_lows, 1)
                    if is_split(g, section):
                        for half in range(2):
                            take_low(halves_until(b, section) + n, n, p, half)
                            n += 1
                    dve.wait_ge(adj_in[p % SLOTS], 16 * (PER_SLOT * b + p // SLOTS + 1))
                    if p == 1:
                        if not first:
                            dve.wait_ge(S["fold_made"], done(b))
                        dve.tensor_tensor(acc[0:ROWS, :], adj_sb[0][0:ROWS, :], adj_sb[1][0:ROWS, :], ALU.add).then_inc(
                            row_sums, 2)
                    if p > 1:
                        dve.wait_ge(row_sums, BLOCKS * b + p)
                        dve.tensor_tensor(acc[0:ROWS, :], acc[0:ROWS, :], adj_sb[p % SLOTS][0:ROWS, :],
                                          ALU.add).then_inc(row_sums, 1)
                dve.wait_ge(row_sums, BLOCKS * (b + 1))
                dve.tensor_tensor(acc[0:ROWS, 0:HALF], acc[0:ROWS, 0:HALF], acc[0:ROWS, HALF:], ALU.add).then_inc(
                    S["fold_half"], 1)
                dve.wait_ge(S["fold_half"], done(b + 1))
                dve.wait_ge(S["u_added"], done(b + 1))
                dve.wait_ge(S["sup_mm"], done(b))
                dve.tensor_tensor(fold[0:ROWS, :], acc[0:ROWS, 0:BLOCK], acc[0:ROWS, BLOCK:HALF], ALU.add).then_inc(
                    S["fold_made"], 1)

            def take_sum(t, v, half):
                dve.wait_ge(halves_used, halves_before(t, v))
                dve.wait_ge(natives_used, natives_before(t, v))
                dve.wait_ge(S["part_in"], loaded(t))
                dve.wait_ge(S["zt_turned"], done(t - 1))
                dve.tensor_tensor(r_t[:, :], z_banks[half][:, 0:BLOCK], part[:, :], ALU.add).then_inc(
                    S["zt_made"], 1)

            def finish(t):
                dve.wait_ge(S["out_stored"], stored(t))
                wait_alone(dve, S["zt_turned"], done(t + 1), waits_passed)
                dve.tensor_copy(dcur[:, :], d_sb[:, bass.ts(BLOCKS - 1 - t, CHUNKS)]).then_inc(S["d_cur"], 1)
                dve.wait_ge(S["d_cur"], done(BLOCKS + t + 1))
                dve.wait_ge(S["x1_in"], loaded(t + 1))
                for c in range(CHUNKS):
                    last = dve.scalar_tensor_tensor(out=normed[:, c, :], in0=ps_r[0:ROWS, c * F:(c + 1) * F],
                                                    scalar=dcur[:, c:c + 1], in1=x1[:, c, :], op0=ALU.mult,
                                                    op1=ALU.add)
                last.then_inc(S["out_made"], 1)

            def pass2(t, v, first, half):
                if first:
                    degrees(BLOCKS - 1)
                    first_residual(BLOCKS - 1)
                    scales(BLOCKS - 1)
                    ln_shift("2", "l2", BLOCKS - 1)
                    support_bias(BLOCKS - 1)
                    second_features(BLOCKS - 1, False)
                    for g in range(WHOLE):
                        dve.wait_ge(held_high, g + 1)
                        dve.tensor_tensor(whole_block(h_low, g), whole_block(s_whole, g),
                                          whole_block(h_high, g).bitcast(F32), ALU.subtract).then_inc(held_low, 1)
                n = 0
                for p, g in enumerate(second_blocks(v)):
                    if p == (2 if v else 0) and not first:
                        take_sum(t, v, 1 - half)
                    if p == (7 if v else 1) and not first:
                        finish(t - 1)
                    if second_split(v, g):
                        for h in range(2):
                            take_low(halves_before(t, v) + n, n, p, h)
                            n += 1

            first_pass(dve, pass1)
            second_pass(dve, pass2)
            take_sum(BLOCKS, SECTIONS - 1, (BLOCKS - 1) % 2)
            finish(BLOCKS - 1)

        @block.tensor
        def _(pe):
            for name in ("u_turned", "u_added", "z1_summed", "r_turned", "h2_turned", "sup_mm", "deg_mm",
                         "zt_turned"):
                pe.sem_inc(S[name], 1)
            pe.wait_ge(bias_rows_in, 32)
            pe.wait_ge(w_item_in, 16)
            pe.wait_ge(consts_set, 4)
            for ps, row in ((ps_u, b_item_row), (ps_h, b_out_row)):
                pe.matmul(ps[0:ROWS, :], ones_row[:, 0:ROWS], row, start=True, stop=True).then_inc(bias_mm, 1)
            for i in range(BLOCKS):
                ps = h_banks[i % 4]
                if i % CHUNKS == 0:
                    pe.wait_ge(item_in[i // CHUNKS], 16)
                if i >= 4:
                    pe.wait_ge(h_sum, i - 3)
                for c in range(CHUNKS):
                    at = (i % CHUNKS * CHUNKS + c) * ROWS
                    last = pe.matmul(ps[0:ROWS, c * F:(c + 1) * F], items[i // CHUNKS][:, at:at + ROWS], w_item,
                                     start=True, stop=True)
                last.then_inc(h_mm, 1)
            pe.wait_ge(consts_in, 48)
            pe.wait_ge(h_low_made, PARTED)
            pe.wait_ge(h_sum, BLOCKS)

            def tile(features, i, c):
                at = (i * CHUNKS + c) * F
                return features[:, at:at + F]

            def native_products(z, features, i, p, starts, ends):
                for c in range(CHUNKS):
                    last = pe.matmul(z[:, 0:BLOCK], tile(features, i, c),
                                     adj_sb[p % SLOTS][0:ROWS, c * BLOCK:(c + 1) * BLOCK],
                                     start=starts and c == 0, stop=ends and c == CHUNKS - 1)
                return last

            def split_products(z, high, low, i, ring, half, starts, ends):
                a_high, a_low = adj_high[ring % RING], adj_low[ring % RING]
                for j in range(CHUNKS // 2):
                    c = half * CHUNKS // 2 + j
                    at = slice(j * BLOCK, (j + 1) * BLOCK)
                    pe.matmul(z[:, 0:BLOCK], tile(high, i, c), a_high[:, at], start=starts and c == 0, stop=False)
                    pe.matmul(z[:, 0:BLOCK], tile(low, i, c), a_high[:, at], start=False, stop=False)
                    last = pe.matmul(z[:, 0:BLOCK], tile(high, i, c), a_low[:, at], start=False,
                                     stop=ends and c == CHUNKS - 1)
                return last

            def turn_rows(ps, src, signal):
                for c in range(CHUNKS):
                    last = pe.transpose(ps[:, c * ROWS:(c + 1) * ROWS], src[:, c, :], ident[0:ROWS, 0:ROWS])
                last.then_inc(S[signal], 1)

            def turn_back(ps, src, signal):
                for c in range(CHUNKS):
                    last = pe.transpose(ps[0:ROWS, c * F:(c + 1) * F], src[:, c * ROWS:(c + 1) * ROWS], ident[:, :])
                last.then_inc(S[signal], 1)

            def degree_sums(e):
                pe.wait_ge(S["fold_made"], done(e + 1))
                pe.wait_ge(S["deg_safe"], done(e))
                for c in range(CHUNKS):
                    last = pe.matmul(ps_d[0:ROWS, c:c + 1], fold[0:ROWS, c * ROWS:(c + 1) * ROWS], ones_col[0:ROWS, :],
                                     start=True, stop=True)
                last.then_inc(S["deg_mm"], 1)

            def turn_r(e):
                pe.wait_ge(S["r_relu"], done(e + 1))
                pe.wait_ge(S["x1_made"], done(e))
                turn_back(ps_r, r_t, "r_turned")

            def turn_h2(e):
                pe.wait_ge(S["h2_norm"], done(e + 1))
                pe.wait_ge(S["h2_relu"], done(e))
                turn_rows(ps_h, normed, "h2_turned")

            def support(e):
                pe.wait_ge(S["h2_relu"], done(e + 1))
                pe.wait_ge(S["sup_bias"], done(e))
                for c in range(CHUNKS):
                    last = pe.matmul(ps_s[0:ROWS, c * F:(c + 1) * F], turned[:, c * ROWS:(c + 1) * ROWS], wo[:, :],
                                     start=True, stop=True)
                last.then_inc(S["sup_mm"], 1)

            def pass1(b, section, first):
                order = column_blocks(section)
                known = SECTION * section
                both = [p for p, g in enumerate(order) if g < known]
                n = 0
                fresh = 0
                if not first:
                    pe.wait_ge(S["r_relu"], done(b))
                for p, g in enumerate(order):
                    ends = p == BLOCKS - 1
                    pe.wait_ge(adj_in[p % SLOTS], 16 * (PER_SLOT * b + p // SLOTS + 1))
                    if p in both[:1]:
                        pe.wait_ge(S["part_made"], done(b - SECTION))
                        pe.wait_ge(S["s_made"], done(known - 1))
                    if ends and section:
                        pe.wait_ge(S["s_made"], done(known))
                    if is_split(g, section):
                        by_layer = [(h_high, h_low, g), (s_high, s_low, g)]
                        for layer, _, _ in fresh_features(g, section):
                            by_layer[layer] = (fresh_high[layer], fresh_low[layer], 0)
                            fresh += 1
                        if g in FRESH[section]:
                            wait_alone(pe, fresh_lows, fresh_before(b, section) + fresh, waits_passed)
                        for half in range(2):
                            pe.wait_ge(lows_made, halves_until(b, section) + n + 1)
                            last = split_products(z1, *by_layer[0], n, half, p == 0, ends)
                            if ends and half and section:
                                last.then_inc(S["z1_summed"], 1)
                            if g < known:
                                last = split_products(z2, *by_layer[1], n, half, p == both[0], ends)
                            last.then_inc(halves_used, 1)
                            n += 1
                    else:
                        h, i = (s_whole, later_whole(g)) if g in LATER else (h_whole, g - PARTED)
                        last = native_products(z1, h, i, p, p == 0, ends)
                        if ends and section:
                            last.then_inc(S["z1_summed"], 1)
                        if g < known:
                            last = native_products(z2, s_whole, g - PARTED, p, p == both[0], ends)
                        last.then_inc(natives_used, 1)
                    if p == 5:
                        pe.wait_ge(S["u_norm"], done(b + 1))
                        pe.wait_ge(S["u_relu"], done(b))
                        turn_rows(ps_u, normed, "u_turned")
                    if p == 9:
                        pe.wait_ge(S["u_relu"], done(b + 1))
                        pe.matmul(z1[:, 0:BLOCK], wu[:, :], turned[:, :], start=False, stop=False).then_inc(
                            S["u_added"], 1)
                    if not first:
                        if p == 1:
                            degree_sums(b - 1)
                        if p == 4:
                            turn_r(b - 1)
                        if p == 10:
                            turn_h2(b - 1)
                        if p == 14:
                            support(b - 1)

            def pass2(t, v, first, half):
                order = second_blocks(v)
                z = z_banks[half]
                if first:
                    degree_sums(BLOCKS - 1)
                    pe.wait_ge(S["r_relu"], done(BLOCKS))
                    pe.wait_ge(S["part_made"], done(BLOCKS - SECTION))
                elif not (v == 0 and t < 2):
                    pe.wait_ge(S["zt_made"], done(t - 1))
                if v == 1:
                    pe.wait_ge(held_low, WHOLE)
                n = 0
                for p, g in enumerate(order):
                    starts, ends = p == 0, p == len(order) - 1
                    pe.wait_ge(adj_in[p % SLOTS], 16 * (second_loads(t, v, p) + 1))
                    if first and ends:
                        support(BLOCKS - 1)
                        pe.wait_ge(S["s_made"], done(BLOCKS))
                    if second_split(v, g):
                        high, low, i = (s_high, s_low, g) if g < PARTED else (h_high, h_low, g - PARTED)
                        for h in range(2):
                            pe.wait_ge(lows_made, halves_before(t, v) + n + 1)
                            split_products(z, high, low, i, n, h, starts, ends).then_inc(halves_used, 1)
                            n += 1
                    else:
                        native_products(z, s_whole, g - PARTED, p, starts, ends).then_inc(natives_used, 1)
                    if first and p == 0:
                        turn_r(BLOCKS - 1)
                    if first and p == 1:
                        turn_h2(BLOCKS - 1)
                    if not first and p == min(3, SECTION * (v + 1) - 3):
                        turn_sum(t - 1)

            def turn_sum(t):
                pe.wait_ge(S["zt_made"], done(t + 1))
                pe.wait_ge(S["out_made"], done(t))
                turn_back(ps_r, r_t, "zt_turned")

            first_pass(pe, pass1)
            second_pass(pe, pass2)
            turn_sum(BLOCKS - 1)


def build(nc, shapes):
    def dram(name, shape, kind="ExternalInput"):
        return nc.dram_tensor(name, shape, F32, kind=kind).ap()

    args = [dram(n, s) for n, s in shapes]
    out = dram("out_0_dram", (BLOCKS, ROWS, CHUNKS * F), "ExternalOutput")
    gnn_two_layers(nc, *args, out)


def kernel(x, adj, L0_gnn_item_feat, L0_gnn_W_item, L0_gnn_b_item, L0_gnn_W_user, L0_gnn_b_user, L1_gnn_W, L1_gnn_b):
    import numpy as np
    import concourse.bacc as bacc
    from concourse.bass_utils import run_bass_kernel_spmd

    def by_chunks(a):
        return np.ascontiguousarray(a.reshape(BLOCKS, CHUNKS, ROWS, F).transpose(0, 2, 1, 3)).reshape(
            BLOCKS, ROWS, CHUNKS * F)

    adj = np.asarray(adj)
    adj_t = np.zeros((BLOCKS, BLOCKS, 128, CHUNKS, BLOCK), adj.dtype)
    adj_t[:, :, :ROWS] = adj.reshape(BLOCKS, BLOCK, BLOCKS, CHUNKS, ROWS).transpose(0, 2, 4, 3, 1)
    arrays = {
        "in_x": by_chunks(np.asarray(x)),
        "in_adj_t": adj_t.reshape(BLOCKS, BLOCKS, 128, GROUP),
        "in_item_t": np.ascontiguousarray(np.asarray(L0_gnn_item_feat).reshape(
            SECTIONS, GROUP, F).transpose(0, 2, 1)),
        "in_w_item_t": np.ascontiguousarray(np.asarray(L0_gnn_W_item).T),
        "in_b_item": np.tile(np.asarray(L0_gnn_b_item), CHUNKS).reshape(1, CHUNKS * F),
        "in_w_user_t": np.ascontiguousarray(np.asarray(L0_gnn_W_user).T),
        "in_b_user": np.asarray(L0_gnn_b_user).reshape(F, 1),
        "in_w_out_t": np.ascontiguousarray(np.asarray(L1_gnn_W).T),
        "in_b_out": np.tile(np.asarray(L1_gnn_b), CHUNKS).reshape(1, CHUNKS * F),
    }
    nc = bacc.Bacc("TRN2", target_bir_lowering=False, num_devices=1, dynamic_dma_scratch_size=SCRATCH)
    build(nc, [(n, a.shape) for n, a in arrays.items()])
    r = run_bass_kernel_spmd(nc, [arrays], core_ids=[0])
    got = r.results[0]["out_0_dram"]
    return got.reshape(BLOCKS, ROWS, CHUNKS, F).transpose(0, 2, 1, 3).reshape(N, F)
```
